# Optimizing a Trainium2 kernel written in Bass

```python
import numpy as np
import jax
import jax.numpy as jnp

def _softmax(x, axis=-1):
    return jax.nn.softmax(x, axis=axis)

def _gelu(x):
    return jax.nn.gelu(x, approximate=True)

def _silu(x):
    return jax.nn.silu(x)

def _sigmoid(x):
    return jax.nn.sigmoid(x)

def _layernorm(x, axis=-1, eps=1e-05):
    m = jnp.mean(x, axis=axis, keepdims=True)
    v = jnp.var(x, axis=axis, keepdims=True)
    return (x - m) / jnp.sqrt(v + eps)

def _scatter_add(tgt, idx, src, axis=0):
    return tgt.at[idx].add(src)

def _segment_sum(src, seg, n):
    return jax.ops.segment_sum(src, seg, n)
kernel_name = 'mk_seq_preln_d1_jaxref_r8_aaf74a'

def setup_inputs(seed: int=0):
    np.random.seed(seed)
    _w = jnp.asarray

    def _L0_attn_setup():
        import jax, jax.numpy as jnp
        import numpy as np
        import math
        N_HEADS, D_HEAD, D_MODEL = (16, 64, 128)
        B, S = (4, 256)
        NEG_MASK = -100000.0
        key = jax.random.key(seed)
        ks = jax.random.split(key, 9)
        bound = math.sqrt(6.0 / (D_MODEL + D_HEAD))

        def w(k):
            return jax.random.uniform(k, (N_HEADS, D_MODEL, D_HEAD), jnp.float32, -bound, bound)
        return {'x': jax.random.normal(ks[0], (B, S, D_MODEL), jnp.float32), 'Q_w': w(ks[1]), 'Q_b': jnp.zeros((N_HEADS, D_HEAD), jnp.float32), 'K_w': w(ks[2]), 'K_b': jnp.zeros((N_HEADS, D_HEAD), jnp.float32), 'V_w': w(ks[3]), 'V_b': jnp.zeros((N_HEADS, D_HEAD), jnp.float32), 'O_w': jax.random.uniform(ks[4], (N_HEADS, D_HEAD, D_MODEL), jnp.float32, -bound, bound), 'O_b': jnp.zeros((D_MODEL,), jnp.float32)}
    _L0_attn_in = _L0_attn_setup()

    def _L0_ffn_setup():
        import jax, jax.numpy as jnp
        import numpy as np
        E = 8
        H = 128
        D = 128
        TOP_K = 2
        key = jax.random.key(seed)
        k0, k1, k2, k3 = jax.random.split(key, 4)
        x = jax.random.normal(k0, (1, 256, H), dtype=jnp.float32)
        router_w = jax.random.normal(k1, (E, H), dtype=jnp.float32) * (1.0 / np.sqrt(H))
        up_proj = jax.random.normal(k2, (E, H, 2 * D), dtype=jnp.float32) * (1.0 / np.sqrt(H))
        down_proj = jax.random.normal(k3, (E, D, H), dtype=jnp.float32) * (1.0 / np.sqrt(D))
        return {'x': x, 'router_w': router_w, 'up_proj': up_proj, 'down_proj': down_proj}
    _L0_ffn_in = _L0_ffn_setup()
    _d = {'L0_attn_x': _L0_attn_in['x'], 'L0_attn_Q_w': _L0_attn_in['Q_w'], 'L0_attn_Q_b': _L0_attn_in['Q_b'], 'L0_attn_K_w': _L0_attn_in['K_w'], 'L0_attn_K_b': _L0_attn_in['K_b'], 'L0_attn_V_w': _L0_attn_in['V_w'], 'L0_attn_V_b': _L0_attn_in['V_b'], 'L0_attn_O_w': _L0_attn_in['O_w'], 'L0_attn_O_b': _L0_attn_in['O_b'], 'L0_ffn_router_w': _L0_ffn_in['router_w'], 'L0_ffn_up_proj': _L0_ffn_in['up_proj'], 'L0_ffn_down_proj': _L0_ffn_in['down_proj']}
    _x0 = _d['L0_attn_x']
    _d['L0_attn_x'] = jax.random.normal(jax.random.fold_in(jax.random.key(seed), 1), (4, 512, 128), dtype=_x0.dtype)
    del _x0
    return _d

def reference(L0_attn_x, L0_attn_Q_w, L0_attn_Q_b, L0_attn_K_w, L0_attn_K_b, L0_attn_V_w, L0_attn_V_b, L0_attn_O_w, L0_attn_O_b, L0_ffn_router_w, L0_ffn_up_proj, L0_ffn_down_proj):

    def _L0_attn_ref(x, Q_w, Q_b, K_w, K_b, V_w, V_b, O_w, O_b):
        import jax, jax.numpy as jnp
        import numpy as np
        import math
        N_HEADS, D_HEAD, D_MODEL = (16, 64, 128)
        B, S = (4, 256)
        NEG_MASK = -100000.0
        q = jnp.einsum('bpm,hmd->bphd', x, Q_w) + Q_b
        k = jnp.einsum('bpm,hmd->bphd', x, K_w) + K_b
        v = jnp.einsum('bpm,hmd->bphd', x, V_w) + V_b
        logits = jnp.einsum('bqhd,bkhd->bhqk', q, k) / math.sqrt(D_HEAD)
        s = logits.shape[-1]
        causal = jnp.triu(jnp.ones((s, s), dtype=bool), k=1)
        logits = jnp.where(causal, NEG_MASK, logits)
        scores = jax.nn.softmax(logits, axis=-1)
        attn = jnp.einsum('bhqk,bkhd->bqhd', scores, v)
        return jnp.einsum('bqhd,hdm->bqm', attn, O_w) + O_b

    def _L0_ffn_ref(x, router_w, up_proj, down_proj):
        import jax, jax.numpy as jnp
        import numpy as np
        E = 8
        H = 128
        D = 128
        TOP_K = 2
        B, T, _ = x.shape
        xt = x.reshape(-1, H)
        N = xt.shape[0]
        logits = jnp.einsum('nh,eh->ne', xt, router_w)
        probs = jax.nn.softmax(logits, axis=-1)
        scores, expert_idx = jax.lax.top_k(probs, TOP_K)
        scores = scores / jnp.sum(scores, axis=-1, keepdims=True)
        gate = jnp.zeros((N, E), dtype=xt.dtype).at[jnp.arange(N)[:, None], expert_idx].add(scores)
        h = jnp.einsum('nh,ehd->end', xt, up_proj)
        hidden = jax.nn.silu(h[..., :D]) * h[..., D:]
        out_e = jnp.einsum('end,edh->enh', hidden, down_proj)
        out = jnp.einsum('ne,enh->nh', gate, out_e)
        return out.reshape(B, T, H)
    x = L0_attn_x
    x = x + _L0_attn_ref(_layernorm(x, axis=-1), L0_attn_Q_w, L0_attn_Q_b, L0_attn_K_w, L0_attn_K_b, L0_attn_V_w, L0_attn_V_b, L0_attn_O_w, L0_attn_O_b)
    x = x + _L0_ffn_ref(_layernorm(x, axis=-1), L0_ffn_router_w, L0_ffn_up_proj, L0_ffn_down_proj)
    return x

_drawn_inputs = setup_inputs


def setup_inputs(seed=0):
    import zlib

    import numpy as np

    out = dict(_drawn_inputs(seed))
    spreads = {'L0_attn_Q_b': (0.0, 0.1),
     'L0_attn_K_b': (0.0, 0.1),
     'L0_attn_V_b': (0.0, 0.1),
     'L0_attn_O_b': (0.0, 0.1)}
    factors = {}
    for name, (base, spread) in spreads.items():
        noise = np.random.default_rng([zlib.crc32(name.encode()), seed]).standard_normal(out[name].shape)
        drawn = base * np.exp(spread * noise) if base else spread * noise
        out[name] = jnp.asarray(drawn.astype(out[name].dtype))
    for name, factor in factors.items():
        out[name] = (out[name] * factor).astype(out[name].dtype)
    return out
```

```python
from contextlib import ExitStack

import concourse.bass as bass
from concourse import mybir

F32 = mybir.dt.float32
F16 = mybir.dt.float16
BF16 = mybir.dt.bfloat16
ALU = mybir.AluOpType
ACT = mybir.ActivationFunctionType
AX_X = mybir.AxisListType.X

P = 128
WS = 16.0
EPS = 1e-5
NEG = -1e30


def build(nc, x, Q_w, Q_b, K_w, K_b, V_w, V_b, O_w, O_b, router_w, up_proj, down_proj, out):
    B, S, D = x.shape
    H, _, DH = Q_w.shape
    E, _, D2 = up_proj.shape
    assert D == P and 2 * DH == P and S == 4 * P and D2 == 2 * P and B == 4
    QT = S // P
    TILES = B * QT
    PAIRS = H // 2
    STEPS = PAIRS * B
    SC = WS * WS * DH ** 0.5
    VW = DH + 1
    MAIN, LAG = 0, 4

    x_t = x.rearrange("b (t p) d -> p (b t) d", p=P)
    out_t = out.rearrange("b (t p) d -> p (b t) d", p=P)

    with ExitStack() as ctx:
        def sem(name):
            return ctx.enter_context(nc.semaphore(name))

        ARENA = 53000
        arena = ctx.enter_context(nc.sbuf_tensor("arena", [P, ARENA], F32))
        at = [0]

        def cut(words):
            a = at[0]
            at[0] += words
            assert at[0] <= ARENA, at[0]
            return a

        def f32(a, *shape):
            n = 1
            for k in shape:
                n *= k
            v = arena[:, a:a + n]
            return v if len(shape) == 1 else v.rearrange(*names(shape), **sizes(shape))

        def f16(a, *shape, dt=F16):
            n = 1
            for k in shape:
                n *= k
            v = arena[:, a:a + (n + 1) // 2].bitcast(dt)[:, 0:n]
            return v if len(shape) == 1 else v.rearrange(*names(shape), **sizes(shape))

        def names(shape):
            ax = "abcdef"[:len(shape)]
            return [f"p ({' '.join(ax)}) -> p {' '.join(ax)}"]

        def sizes(shape):
            return {"abcdef"[i]: k for i, k in enumerate(shape) if i}

        identf = f32(cut(P), P)
        mask = f16(cut(S // 2), S, dt=BF16)
        cols = f32(cut(32), 4, PAIRS)
        routh = f16(cut(E // 2), E)
        routl = f16(cut(E // 2), E)
        stats = f32(cut(TILES * 6), TILES, 6)
        mv = f32(cut(TILES * 2), TILES, 2)
        rstd = f32(cut(TILES), TILES)
        xTh = f16(cut(TILES * P // 2), TILES * P)
        xTl = f16(cut(TILES * P // 2), TILES * P)
        wqh, wql, wkh, wkl = (f16(cut(H * DH // 2), PAIRS, P) for _ in range(4))
        v_at = cut(TILES * H * VW // 2 + TILES * H * DH // 2)
        Vh = f16(v_at, TILES, H, VW)
        Vl = f16(v_at + TILES * H * VW // 2, TILES, H, DH)
        at_at = cut(PAIRS * TILES * P)
        ATh = f16(at_at, PAIRS, B, S)
        ATl = f16(at_at + PAIRS * TILES * P // 2, PAIRS, B, S)
        stack_at = cut(2 * 2 * 4 * S // 2)
        KLO, KHI, QHL, QSH = range(4)
        stack = f16(stack_at, 2, 2, 4, S)
        src_at = cut(2 * 4 * S // 2)
        halves = f16(src_at, 2, 4, S)
        p32_at = cut(4 * S)
        P32 = f32(p32_at, 4, S)
        ph_at = cut(2 * 2 * 5 * S // 2)
        Ph = f16(ph_at, 2, 5, S)
        Pl = f16(ph_at + 2 * 5 * S // 2, 2, 5, S)
        junk = f16(cut(S), 2, S, dt=BF16)
        mneg = f32(cut(16), 2, 8)
        mrow = f16(cut(P), 2, P)
        rec = f32(cut(8), 8)
        dummy = f32(cut(4), 4)
        bias = f32(cut(4), 3)
        An = f32(cut(S), QT, P)

        xraw = f32(at_at, TILES, P)
        wraw = [f32(at_at + TILES * P + i * H * DH, PAIRS, P) for i in range(3)]
        xn = f32(at_at + TILES * P + 3 * H * DH, TILES, P)
        small = f32(at_at + 2 * TILES * P + 3 * H * DH, P)
        wvh = f16(ph_at, H * DH)
        wvl = f16(ph_at + H * DH // 2, H * DH)

        raw2 = f32(v_at, 4 * 1024)
        oraw = raw2[:, 0:PAIRS * P]
        upraw = raw2[:, 1024:1024 + E * D2]
        dnraw = raw2[:, 3072:3072 + E * P]
        w2_at = v_at + 4096
        oh, ol = (f16(w2_at + i * 512, PAIRS, P) for i in range(2))
        uph, upl = (f16(w2_at + 1024 + i * 1024, E, D2) for i in range(2))
        dnh, dnl = (f16(w2_at + 3072 + i * 512, E, P) for i in range(2))
        x1 = f32(w2_at + 4096, TILES, P)
        xn2 = f32(w2_at + 4096 + 2048, TILES, P)
        xres = f32(stack_at, TILES, P)
        obb = f32(stack_at + 2048, P)
        xob = f32(stack_at + 2048 + P, TILES, P)
        sil = f32(p32_at, 2, S)
        h32 = f32(p32_at + 2 * S, 2, S)
        hh = f16(ph_at, 4, S)
        hl = f16(ph_at + 4 * S // 2, 4, S)
        gl_at = ph_at + 4 * S
        G = [f32(gl_at + i * TILES * E, TILES, E) for i in range(8)]
        g1 = [f32(gl_at + 8 * TILES * E + i * TILES, TILES) for i in range(4)]
        assert gl_at + 8 * TILES * E + 4 * TILES < at[0] and stack_at + 4096 + P <= p32_at

        bank = [ctx.enter_context(nc.psum_tensor(f"bank{i}", [P, 512], F32)) for i in range(8)]
        proj_b = bank[0:2]
        st_b = bank[2:4]
        sn_b = bank[4:6]
        o_b = bank[6:8]

        x_in = [sem(f"x_in{b}") for b in range(B)]
        w_in = [sem(f"w_in{i}") for i in range(3)]
        small_in = sem("small_in")
        ident_done, const_done = sem("ident_done"), sem("const_done")
        stat_done, ln_done = sem("stat_done"), sem("ln_done")
        sd_done, rs_done = sem("sd_done"), sem("rs_done")
        xt_mm, xh_done, xl_done = sem("xt_mm"), sem("xh_done"), sem("xl_done")
        cols_mm, cols_done = sem("cols_mm"), sem("cols_done")
        wh_done, wl_done = sem("wh_done"), sem("wl_done")
        v_mm, vh_done, vl_done = sem("v_mm"), sem("vh_done"), sem("vl_done")
        qkbias_done, vbias_done = sem("qkbias_done"), sem("vbias_done")
        proj_mm, hi_done, lo_done = sem("proj_mm"), sem("hi_done"), sem("lo_done")
        dup_done = [sem("dup_done0"), sem("dup_done1")]
        shift_in = [sem("shift_in0"), sem("shift_in1")]
        sn_mm, max_done, mt_mm, mrow_done = sem("sn_mm"), sem("max_done"), sem("mt_mm"), sem("mrow_done")
        st_mm, exp_done, tri_done = sem("st_mm"), sem("exp_done"), sem("tri_done")
        pha_done, phd_done, pl_done = sem("pha_done"), sem("phd_done"), sem("pl_done")
        av_mm, rec_done, norm_done = sem("av_mm"), sem("rec_done"), sem("norm_done")
        at_mm, ath_done, atl_done = sem("at_mm"), sem("ath_done"), sem("atl_done")
        x2_in, w2_in = sem("x2_in"), [sem(f"w2_in{i}") for i in range(3)]
        w2h_done, w2l_done = sem("w2h_done"), sem("w2l_done")
        xob_done = sem("xob_done")
        o_mm, x1_done = sem("o_mm"), sem("x1_done")
        stat2_done, sd2_done, rs2_done, ln2_done = sem("stat2_done"), sem("sd2_done"), sem("rs2_done"), sem("ln2_done")
        x2t_mm, x2h_done, x2l_done = sem("x2t_mm"), sem("x2h_done"), sem("x2l_done")
        rout_mm, chain, gexp_in, gexp_done, gate_done = (
            sem("rout_mm"), sem("chain"), sem("gexp_in"), sem("gexp_done"), sem("gate_done"))
        up_mm, sil_done, h_done, hh_done, hl_done = (
            sem("up_mm"), sem("sil_done"), sem("h_done"), sem("hh_done"), sem("hl_done"))
        dn_mm, acc_done, out_done = sem("dn_mm"), sem("acc_done"), sem("out_done")

        def count(n, per, plus):
            k, c = n
            return k * (B * per) + (per * c + plus)

        def halfcount(n, per, plus):
            k, c = n
            return k * (B // 2 * per) + (per * (c // 2) + plus)

        def wait(eng, s, value):
            if not isinstance(value, int) or value > 0:
                eng.wait_ge(s, value)

        def live(n):
            k, c = n
            return not isinstance(k, int) or 0 <= B * k + c < STEPS

        def minus(n, d):
            return (n[0], n[1] - d)

        def where(n):
            k, c = n
            return k + c // B, c % B

        def pipeline(eng, step):
            for b in range(B):
                step((0, b))
            with eng.Fori(1, PAIRS) as k:
                for b in range(B):
                    step((k, b))
            for b in range(LAG):
                step((PAIRS, b))

        def pipeline_moe(eng, step, lag):
            for c in range(B):
                step((0, c))
            with eng.Fori(1, E) as e:
                for c in range(B):
                    step((e, c))
            for c in range(lag):
                step((E, c))

        SN = [[(0, 3, 0)], [(0, 2, 0), (0, 0, 384)], [(1, 3, 0)], [(1, 2, 0), (1, 0, 384)], [(0, 1, 0), (1, 1, 256)]]
        SN_CUM = [1, 3, 4, 6, 8]
        ST = [[(0, 0, 0)], [(0, 1, 0), (0, 3, 384)], [(1, 0, 0)], [(1, 1, 0), (1, 3, 384)], [(0, 2, 0), (1, 2, 256)]]
        PH_ACT = [0, 2, 4]

        def ph_wait(eng, n, u):
            if u in PH_ACT:
                eng.wait_ge(pha_done, count(n, len(PH_ACT), PH_ACT.index(u) + 1))
            else:
                rest = [w for w in range(5) if w not in PH_ACT]
                eng.wait_ge(phd_done, count(n, len(rest), rest.index(u) + 1))

        def p_block(tile, n, head, j, i):
            for u, parts in enumerate(ST):
                for h, key_tile, first in parts:
                    if h == head and key_tile == j:
                        a = first + (i - j) * P
                        return tile[:, n[1] % 2, u, a:a + P]

        block = ctx.enter_context(nc.Block())

        @block.sync
        def _(sp):
            for b in range(B):
                sp.dma_start(xraw[:, QT * b:QT * b + QT, :], x_t[:, QT * b:QT * b + QT, :]).then_inc(x_in[b], 16)
                if b == 0:
                    sp.dma_start(small[0:8, :], Q_b.rearrange("(a h) d -> a (h d)", h=2)).then_inc(small_in, 16)
                    sp.dma_start(small[8:16, :], K_b.rearrange("(a h) d -> a (h d)", h=2)).then_inc(small_in, 16)
                    sp.dma_start(small[16:24, :], V_b.rearrange("(a h) d -> a (h d)", h=2)).then_inc(small_in, 16)
                    sp.dma_start(small[24:32, :], router_w).then_inc(small_in, 16)
            for i, w in enumerate((V_w, Q_w, K_w)):
                sp.dma_start(wraw[i].rearrange("p a (h d) -> p (a h) d", h=2),
                             w.rearrange("h m d -> m h d")).then_inc(w_in[i], 16)

            def step(s):
                if live(s):
                    k, c = s
                    r = c % 2
                    if isinstance(k, int) and c == 0:
                        sp.wait_ge(lo_done, 2)
                    else:
                        sp.wait_ge(max_done, count(s, 8, -8 + SN_CUM[2] + 1))
                    for h in range(2):
                        own, other = slice(DH * h, DH * h + DH), slice(DH - DH * h, P - DH * h)
                        sp.dma_start(stack[own, r, h, 0:3, :], halves[own, r, 0:3, :]).then_inc(dup_done[r], 16)
                        sp.dma_start(stack[own, r, h, QSH, :], halves[own, r, 2, :]).then_inc(dup_done[r], 16)
                        sp.dma_start(stack[other, r, h, 1:3, :], halves[own, r, 1:4:2, :]).then_inc(dup_done[r], 16)
                m = minus(s, 1)
                if live(m):
                    r = m[1] % 2
                    sp.wait_ge(mrow_done, count(m, 1, 1))
                    for h in range(2):
                        row = DH - DH * h
                        sp.dma_start(stack[row:row + 1, r, h, QSH, :].rearrange("p (t q) -> p t q", t=QT),
                                     mrow[QT * h:QT * h + QT, r, :]).then_inc(shift_in[r], 16)

            sp.wait_ge(const_done, 1)
            pipeline(sp, step)

            sp.wait_ge(av_mm, 2 * STEPS)
            sp.dma_start(oraw.rearrange("p (a m) -> p a m", a=PAIRS),
                         O_w.rearrange("(a h) d m -> (h d) a m", h=2)).then_inc(w2_in[0], 16)
            sp.dma_start(xres[:, :, :], x_t).then_inc(x2_in, 16)
            sp.dma_start(obb[:, :], O_b.rearrange("(a m) -> a m", a=1).broadcast_to([P, D])).then_inc(x2_in, 16)
            sp.dma_start(upraw.rearrange("p (e n) -> p e n", e=E), up_proj.rearrange("e h n -> h e n")).then_inc(w2_in[1], 16)
            sp.dma_start(dnraw.rearrange("p (e n) -> p e n", e=E), down_proj.rearrange("e h n -> h e n")).then_inc(w2_in[2], 16)
            for b in range(B):
                sp.wait_ge(acc_done, 4 * B * (E - 1) + 4 * (b + 1))
                sp.dma_start(out_t[:, QT * b:QT * b + QT, :], x1[:, QT * b:QT * b + QT, :]).then_inc(out_done, 16)
            sp.wait_ge(out_done, 16 * B)

        @block.gpsimd
        def _(pool):
            g = nc.gpsimd
            g.memset(identf, 0.0).then_inc(ident_done, 1)
            pool.wait_ge(ident_done, 1)
            g.affine_select(out=identf, in_=identf, compare_op=ALU.not_equal, fill=1.0, base=0,
                            pattern=[[-1, P]], channel_multiplier=1).then_inc(ident_done, 1)
            pool.wait_ge(ident_done, 2)
            g.memset(mask, 0.0).then_inc(ident_done, 1)
            pool.wait_ge(ident_done, 3)
            g.affine_select(out=mask[:, S - P:S], in_=mask[:, S - P:S], compare_op=ALU.is_ge, fill=NEG, base=0,
                            pattern=[[-1, P]], channel_multiplier=1).then_inc(ident_done, 1)
            pool.wait_ge(ident_done, 4)
            g.memset(dummy, 0.0).then_inc(ident_done, 1)
            pool.wait_ge(ident_done, 5)
            g.memset(Vh[:, :, :, DH:VW], 1.0).then_inc(ident_done, 1)
            for h in range(2):
                other = slice(DH - DH * h, P - DH * h)
                row = DH - DH * h
                pool.wait_ge(ident_done, 6 + 3 * h)
                g.memset(stack[other, :, h, KLO, :], 0.0).then_inc(ident_done, 1)
                pool.wait_ge(ident_done, 7 + 3 * h)
                g.memset(stack[other, :, h, QSH, :], 0.0).then_inc(ident_done, 1)
                pool.wait_ge(ident_done, 8 + 3 * h)
                g.memset(stack[row:row + 1, :, h, KLO, :], SC).then_inc(ident_done, 1)
            pool.wait_ge(ident_done, 12)
            g.memset(dummy[:, 1:2], 0.0).then_inc(const_done, 1)
            pool.wait_ge(const_done, 1)

            def tri(m, u):
                slot = (5 * m[1] + u) % 4
                parts = ST[u]
                if len(parts) == 1:
                    v = P32[:, slot, 0:P]
                    pat = [[1, P]]
                else:
                    a = parts[1][2]
                    v = P32[:, slot, :].rearrange("p (a q) -> p a q", q=P)[:, 0:a // P + 1:a // P, :]
                    pat = [[0, 2], [1, P]]
                pool.wait_ge(exp_done, count(m, 5, u + 1))
                wait(pool, tri_done, count(m, 5, u))
                g.tensor_tensor(dummy[0:1, 1:2], dummy[0:1, 0:1], dummy[0:1, 0:1], ALU.add)
                g.affine_select(out=v, in_=v, compare_op=ALU.is_ge, fill=0.0, base=0, pattern=pat,
                                channel_multiplier=-1).then_inc(tri_done, 1)

            def low(m, u):
                slot = (5 * m[1] + u) % 4
                r = m[1] % 2
                if u == 0:
                    wait(pool, av_mm, count(m, 2, -2))
                ph_wait(pool, m, u)
                g.tensor_tensor(Pl[:, r, u, :], P32[:, slot, :], Ph[:, r, u, :], ALU.subtract).then_inc(pl_done, 1)

            def step(s):
                m = minus(s, 2)
                if live(m):
                    tri(m, 0)
                    for u in range(5):
                        if u < 4:
                            tri(m, u + 1)
                        low(m, u)

            pipeline(pool, step)

            pool.wait_ge(x2_in, 32)
            for t in range(TILES):
                g.tensor_tensor(xob[:, t, :], xres[:, t, :], obb[:, :], ALU.add).then_inc(xob_done, 1)

            def moe(n):
                if live(n):
                    pool.wait_ge(hh_done, count(n, 1, 1))
                    wait(pool, dn_mm, count(n, 1, -3))
                    g.tensor_tensor(hl[:, n[1] % 4, :], h32[:, n[1] % 2, :], hh[:, n[1] % 4, :],
                                    ALU.subtract).then_inc(hl_done, 1)

            for c in range(B):
                moe((0, c))
            with pool.Fori(1, E) as e:
                for c in range(B):
                    moe((e, c))

        @block.scalar
        def _(act):
            a = nc.scalar
            for i, dst in enumerate((wvh, wqh, wkh)):
                src = wraw[i].rearrange("p a n -> p (a n)")
                d = dst if i == 0 else dst.rearrange("p a n -> p (a n)")
                if i == 1:
                    act.wait_ge(stat_done, 2 * TILES + 1)
                    a.activation(rstd, rstd, ACT.Sqrt).then_inc(sd_done, 1)
                act.wait_ge(w_in[i], 16)
                a.activation(d, src, ACT.Identity, scale=WS).then_inc(wh_done, 1)
            act.wait_ge(cols_mm, 1)
            a.activation(cols.rearrange("p a n -> p (a n)"), bank[4][:, 0:32], ACT.Identity, scale=WS).then_inc(cols_done, 1)
            act.wait_ge(cols_done, 1)
            a.activation(routh, cols[:, 3, :], ACT.Identity).then_inc(cols_done, 1)
            for b in range(B):
                act.wait_ge(xt_mm, b + 1)
                a.activation(xTh[:, S * b:S * b + S], bank[b][:, :], ACT.Identity).then_inc(xh_done, 1)

            def vhalf(t, half, c):
                act.wait_ge(v_mm, c)
                act.wait_ge(const_done, 1)
                a.activation(Vh[:, t, 8 * half:8 * half + 8, 0:DH],
                             bank[4 + half][:, :].rearrange("p (h d) -> p h d", h=8), ACT.Identity).then_inc(vh_done, 1)

            with act.Fori(0, TILES) as t:
                for half in range(2):
                    vhalf(t, half, t * 2 + half + 1)

            def expo(m, u):
                idx = 5 * m[1] + u
                act.wait_ge(st_mm, count(m, 5, u + 1))
                wait(act, pl_done, count(m, 5, u - 3))
                a.activation(P32[:, idx % 4, :], st_b[idx % 2][:, :], ACT.Exp, scale=1.0 / SC).then_inc(exp_done, 1)

            def high(m, u):
                idx = 5 * m[1] + u
                if u == PH_ACT[0]:
                    wait(act, av_mm, count(m, 2, -2))
                act.wait_ge(tri_done, count(m, 5, u + 1))
                a.activation(Ph[:, m[1] % 2, u, :], P32[:, idx % 4, :], ACT.Identity).then_inc(pha_done, 1)

            def step(s):
                if live(s):
                    k, _ = where(s)
                    r = s[1] % 2
                    if s[1] == 0:
                        act.wait_ge(qkbias_done, k + 1)
                    for i, kind in enumerate((2, 1)):
                        act.wait_ge(proj_mm, count(s, 2, i + 1))
                        if i == 0:
                            wait(act, dup_done[r], halfcount(s, 96, 0))
                        a.activation(halves[:, r, kind, :], proj_b[i][:, :], ACT.Identity,
                                     bias=bias[:, i:i + 1]).then_inc(hi_done, 1)
                m = minus(s, 2)
                w = minus(s, 1)
                t = minus(s, 4)
                if live(m):
                    expo(m, 0)
                    expo(m, 1)
                    high(m, 0)
                    expo(m, 2)
                    expo(m, 3)
                    high(m, 2)
                if live(t):
                    k, b = where(t)
                    if b == 0:
                        act.wait_ge(vbias_done, k + 1)
                    act.wait_ge(at_mm, count(t, 1, 1))
                if live(m):
                    expo(m, 4)
                elif live(t):
                    a.activation(dummy[0:1, 2:3], dummy[0:1, 0:1], ACT.Identity)
                if live(t):
                    a.activation(ATh[:, k, b, :], proj_b[0][:, :], ACT.Identity,
                                 bias=bias[:, 2:3]).then_inc(ath_done, 1)
                if live(w):
                    r = w[1] % 2
                    act.wait_ge(mt_mm, count(w, 1, 1))
                    wait(act, shift_in[r], halfcount(w, 32, 0))
                    a.activation(mrow[0:8, r, :], sn_b[(5 * w[1] + 4) % 2][0:8, 0:P], ACT.Identity).then_inc(mrow_done, 1)
                if live(m):
                    high(m, 4)

            act.wait_ge(const_done, 1)
            pipeline(act, step)

            for i, (raw, dst) in enumerate(((oraw, oh), (upraw, uph), (dnraw, dnh))):
                act.wait_ge(w2_in[i], 16)
                a.activation(dst.rearrange("p a n -> p (a n)"), raw, ACT.Identity, scale=WS).then_inc(w2h_done, 1)
            for b in range(B):
                act.wait_ge(stat2_done, 9 * (b + 1))
                a.activation(rstd[:, QT * b:QT * b + QT], rstd[:, QT * b:QT * b + QT], ACT.Sqrt).then_inc(sd2_done, 1)
                act.wait_ge(x2t_mm, b + 1)
                a.activation(xTh[:, S * b:S * b + S], bank[2 + b % 2][:, :], ACT.Identity).then_inc(x2h_done, 1)
            act.wait_ge(gexp_in, 1)
            a.activation(G[2], G[1], ACT.Exp).then_inc(gexp_done, 1)

            def silu(n):
                act.wait_ge(up_mm, count(n, 2, 1))
                wait(act, h_done, count(n, 1, -1))
                a.activation(sil[:, n[1] % 2, :], bank[n[1] % 2][:, :], ACT.Silu, scale=1.0 / WS).then_inc(sil_done, 1)

            def hhigh(n):
                act.wait_ge(h_done, count(n, 1, 1))
                wait(act, dn_mm, count(n, 1, -3))
                a.activation(hh[:, n[1] % 4, :], h32[:, n[1] % 2, :], ACT.Identity).then_inc(hh_done, 1)

            def moe(n):
                if live(n):
                    silu(n)
                m = minus(n, 1)
                if live(m):
                    hhigh(m)

            pipeline_moe(act, moe, 1)

        @block.vector
        def _(dve):
            v = nc.vector
            links = [0]

            def link(ins):
                links[0] += 1
                ins.then_inc(chain, 1)
                dve.wait_ge(chain, links[0])

            def layernorm_stats(b, src, done):
                for t in range(QT * b, QT * b + QT):
                    v.bn_stats(stats[:, t, :], src[:, t, :]).then_inc(done, 1)

            for b in range(B):
                dve.wait_ge(x_in[b], 16)
                layernorm_stats(b, xraw, stat_done)
                dve.wait_ge(stat_done, 2 * QT * b + QT)
                for t in range(QT * b, QT * b + QT):
                    v.bn_aggr(mv[:, t, :], stats[:, t, :]).then_inc(stat_done, 1)
            dve.wait_ge(stat_done, 2 * TILES)
            v.tensor_scalar(rstd, mv[:, :, 1], EPS, None, ALU.add).then_inc(stat_done, 1)
            dve.wait_ge(wh_done, 1)
            v.scalar_tensor_tensor(wvl, wraw[0].rearrange("p a n -> p (a n)"), WS, wvh,
                                   ALU.mult, ALU.subtract).then_inc(wl_done, 1)
            dve.wait_ge(sd_done, 1)
            v.reciprocal(rstd, rstd).then_inc(rs_done, 1)
            dve.wait_ge(rs_done, 1)
            for t in range(TILES):
                v.tensor_scalar(xn[:, t, :], xraw[:, t, :], mv[:, t, 0:1], rstd[:, t:t + 1],
                                ALU.subtract, ALU.mult).then_inc(ln_done, 1)
            for b in range(B):
                dve.wait_ge(xh_done, b + 1)
                v.tensor_tensor(xTl[:, S * b:S * b + S], bank[b][:, :], xTh[:, S * b:S * b + S],
                                ALU.subtract).then_inc(xl_done, 1)
            dve.wait_ge(cols_done, 2)
            v.tensor_tensor(routl, cols[:, 3, :], routh, ALU.subtract).then_inc(cols_done, 1)
            for i, (hi, lo) in enumerate(((wqh, wql), (wkh, wkl))):
                dve.wait_ge(wh_done, 2 + i)
                v.scalar_tensor_tensor(lo.rearrange("p a n -> p (a n)"), wraw[1 + i].rearrange("p a n -> p (a n)"), WS,
                                       hi.rearrange("p a n -> p (a n)"), ALU.mult, ALU.subtract).then_inc(wl_done, 1)

            with dve.Fori(0, TILES) as t:
                for half in range(2):
                    dve.wait_ge(vh_done, t * 2 + half + 1)
                    v.tensor_tensor(Vl[:, t, 8 * half:8 * half + 8, :],
                                    bank[4 + half][:, :].rearrange("p (h d) -> p h d", h=8),
                                    Vh[:, t, 8 * half:8 * half + 8, 0:DH], ALU.subtract).then_inc(vl_done, 1)

            def maxima(m, g):
                r = m[1] % 2
                if g == 0:
                    wait(dve, mt_mm, count(m, 1, -1))
                dve.wait_ge(sn_mm, count(m, 5, g + 1))
                idx = 5 * m[1] + g
                wait(dve, max_done, count(m, 8, ([0] + SN_CUM)[g]))
                v.memset(dummy[:, 3:4], 0.0)
                for h, i, first in SN[g]:
                    n = P * (i + 1)
                    v.tensor_tensor_reduce(junk[:, idx % 2, first:first + n], sn_b[idx % 2][:, first:first + n],
                                           mask[:, S - n:S], -1.0 / SC, 3e38, ALU.add, ALU.min,
                                           mneg[:, r, QT * h + i:QT * h + i + 1]).then_inc(max_done, 1)

            def high(m, u):
                dve.wait_ge(tri_done, count(m, 5, u + 1))
                if u == 1:
                    wait(dve, av_mm, count(m, 2, -2))
                v.tensor_copy(Ph[:, m[1] % 2, u, :], P32[:, (5 * m[1] + u) % 4, :]).then_inc(phd_done, 1)

            def step(s):
                t = minus(s, 4)
                if live(t):
                    dve.wait_ge(av_mm, count(t, 2, 2))
                    wait(dve, norm_done, count(t, 2, 0))
                    k, b = where(t)
                    if b == 0:
                        wait(dve, ath_done, count(t, 1, 0))
                        wait(dve, atl_done, count(t, 1, 0))
                        v.tensor_scalar(bias[:, 2:3], cols[:, 2, bass.ds(k, 1)], 1.0, None,
                                        ALU.mult).then_inc(vbias_done, 1)
                    for h in range(2):
                        v.reciprocal(rec[:, QT * h:QT * h + QT],
                                     o_b[h][:, 0:QT * VW].rearrange("p (t c) -> p t c", t=QT)[:, :, DH]).then_inc(rec_done, 1)
                    dve.wait_ge(rec_done, count(t, 2, 2))
                    wait(dve, at_mm, count(t, 1, 0))
                    for h in range(2):
                        v.tensor_tensor(An[:, :, DH * h:DH * h + DH],
                                        o_b[h][:, 0:QT * VW].rearrange("p (t c) -> p t c", t=QT)[:, :, 0:DH],
                                        rec[:, QT * h:QT * h + QT].unsqueeze(2).broadcast_to([P, QT, DH]),
                                        ALU.mult).then_inc(norm_done, 1)
                if live(s):
                    k, _ = where(s)
                    r = s[1] % 2
                    if s[1] == 0:
                        wait(dve, hi_done, count(s, 2, 0))
                        v.tensor_scalar(bias[:, 0:2], cols[:, 0:2, bass.ds(k, 1)].rearrange("p a n -> p (a n)"),
                                        1.0, None, ALU.mult).then_inc(qkbias_done, 1)
                        dve.wait_ge(qkbias_done, k + 1)
                    for i, (hi, lo) in enumerate(((2, 3), (1, 0))):
                        if i == 0:
                            wait(dve, dup_done[r], halfcount(s, 96, 0))
                        dve.wait_ge(hi_done, count(s, 2, i + 1))
                        v.scalar_tensor_tensor(halves[:, r, lo, :], proj_b[i][:, :], bias[:, i:i + 1],
                                               halves[:, r, hi, :], ALU.add, ALU.subtract).then_inc(lo_done, 1)
                w = minus(s, 1)
                m = minus(s, 2)
                if live(w):
                    maxima(w, 0)
                    maxima(w, 1)
                if live(m):
                    high(m, 1)
                if live(w):
                    maxima(w, 2)
                if live(t):
                    k, b = where(t)
                    dve.wait_ge(ath_done, count(t, 1, 1))
                    v.scalar_tensor_tensor(ATl[:, k, b, :], proj_b[0][:, :], bias[:, 2:3],
                                           ATh[:, k, b, :], ALU.add, ALU.subtract).then_inc(atl_done, 1)
                if live(w):
                    maxima(w, 3)
                    maxima(w, 4)
                if live(m):
                    high(m, 3)

            dve.wait_ge(const_done, 1)
            pipeline(dve, step)

            for i, (raw, hi, lo) in enumerate(((oraw, oh, ol), (upraw, uph, upl), (dnraw, dnh, dnl))):
                dve.wait_ge(w2h_done, i + 1)
                v.scalar_tensor_tensor(lo.rearrange("p a n -> p (a n)"), raw, WS, hi.rearrange("p a n -> p (a n)"),
                                       ALU.mult, ALU.subtract).then_inc(w2l_done, 1)
            dve.wait_ge(xob_done, TILES)
            for b in range(B):
                tiles = slice(QT * b, QT * b + QT)
                dve.wait_ge(o_mm, QT * (b + 1))
                v.scalar_tensor_tensor(x1[:, tiles, :], bank[b % 2][:, :].rearrange("p (t d) -> p t d", t=QT),
                                       1.0 / (WS * WS), xob[:, tiles, :], ALU.mult, ALU.add).then_inc(x1_done, 1)
                dve.wait_ge(x1_done, b + 1)
                layernorm_stats(b, x1, stat2_done)
                dve.wait_ge(stat2_done, 9 * b + QT)
                for t in range(QT * b, QT * b + QT):
                    v.bn_aggr(mv[:, t, :], stats[:, t, :]).then_inc(stat2_done, 1)
                dve.wait_ge(stat2_done, 9 * b + 2 * QT)
                v.tensor_scalar(rstd[:, tiles], mv[:, tiles, 1], EPS, None, ALU.add).then_inc(stat2_done, 1)
                dve.wait_ge(sd2_done, b + 1)
                v.reciprocal(rstd[:, tiles], rstd[:, tiles]).then_inc(rs2_done, 1)
                dve.wait_ge(rs2_done, b + 1)
                for t in range(QT * b, QT * b + QT):
                    v.tensor_scalar(xn2[:, t, :], x1[:, t, :], mv[:, t, 0:1], rstd[:, t:t + 1],
                                    ALU.subtract, ALU.mult).then_inc(ln2_done, 1)
                dve.wait_ge(x2h_done, b + 1)
                v.tensor_tensor(xTl[:, S * b:S * b + S], bank[2 + b % 2][:, :], xTh[:, S * b:S * b + S],
                                ALU.subtract).then_inc(x2l_done, 1)

            def over_e(t):
                return t.unsqueeze(2).broadcast_to([P, TILES, E])

            dve.wait_ge(rout_mm, TILES)
            link(v.tensor_scalar(G[0], bank[7][:, 0:TILES * E].rearrange("p (t e) -> p t e", e=E),
                                 1.0 / WS, None, ALU.mult))
            for e in range(E):
                v.memset(G[7][:, :, e], float(E - e)).then_inc(chain, 1)
            links[0] += E
            link(v.tensor_reduce(g1[0], G[0], AX_X, ALU.max))
            link(v.tensor_tensor(G[1], G[0], over_e(g1[0]), ALU.subtract))
            v.tensor_copy(G[6], G[1]).then_inc(gexp_in, 1)
            dve.wait_ge(gexp_in, 1)

            def pick(values, onehot):
                link(v.tensor_reduce(g1[1], values, AX_X, ALU.max))
                link(v.tensor_tensor(G[4], values, over_e(g1[1]), ALU.is_ge))
                link(v.tensor_tensor(G[4], G[4], G[7], ALU.mult))
                link(v.tensor_reduce(g1[2], G[4], AX_X, ALU.max))
                link(v.tensor_tensor(onehot, G[4], over_e(g1[2]), ALU.is_ge))

            pick(G[6], G[3])
            link(v.tensor_scalar(G[5], G[3], NEG, None, ALU.mult))
            link(v.tensor_tensor(G[6], G[6], G[5], ALU.add))
            pick(G[6], G[5])
            link(v.tensor_tensor(G[3], G[3], G[5], ALU.add))
            dve.wait_ge(gexp_done, 1)
            link(v.tensor_tensor(G[4], G[2], G[3], ALU.mult))
            link(v.tensor_reduce(g1[1], G[4], AX_X, ALU.add))
            link(v.tensor_scalar(g1[2], g1[1], WS * WS, None, ALU.mult))
            link(v.reciprocal(g1[3], g1[2]))
            v.tensor_tensor(G[0], G[4], over_e(g1[3]), ALU.mult).then_inc(gate_done, 1)
            dve.wait_ge(gate_done, 1)

            def moe(n):
                if live(n):
                    dve.wait_ge(up_mm, count(n, 2, 2))
                    wait(dve, hl_done, count(n, 1, -1))
                    dve.wait_ge(sil_done, count(n, 1, 1))
                    v.tensor_tensor(h32[:, n[1] % 2, :], bank[2 + n[1] % 2][:, :], sil[:, n[1] % 2, :],
                                    ALU.mult).then_inc(h_done, 1)
                m = minus(n, 2)
                if live(m):
                    e, b = where(m)
                    dve.wait_ge(dn_mm, count(m, 1, 1))
                    wait(dve, acc_done, count(m, 4, -8))
                    for t in range(QT):
                        tile = QT * b + t
                        v.scalar_tensor_tensor(x1[:, tile, :], bank[4 + m[1] % 2][:, P * t:P * t + P],
                                               G[0][:, tile, bass.ds(e, 1)], x1[:, tile, :],
                                               ALU.mult, ALU.add).then_inc(acc_done, 1)

            pipeline_moe(dve, moe, 2)

        @block.tensor
        def _(pe):
            def three(dst, ah, al, bh, bl, first=True, last=True):
                pe.matmul(dst, ah, bh, start=first, stop=False)
                pe.matmul(dst, ah, bl, start=False, stop=False)
                return pe.matmul(dst, al, bh, start=False, stop=last)

            pe.wait_ge(small_in, 64)
            pe.wait_ge(ident_done, 2)
            pe.transpose(bank[4][:, 0:32], small[0:32, :], identf[0:32, 0:32]).then_inc(cols_mm, 1)
            for b in range(B):
                pe.wait_ge(ln_done, QT * (b + 1))
                for t in range(QT):
                    mm = pe.transpose(bank[b][:, P * t:P * t + P], xn[:, QT * b + t, :], identf)
                mm.then_inc(xt_mm, 1)

            pe.wait_ge(cols_done, 1)
            pe.wait_ge(wl_done, 1)
            pe.wait_ge(xh_done, B)
            pe.wait_ge(xl_done, B)

            def values(t, half, free):
                wait(pe, vl_done, free)
                tok = bass.ts(t, P)
                cs = slice(512 * half, 512 * half + 512)
                three(bank[4 + half][:, :], xTh[:, tok], xTl[:, tok], wvh[:, cs], wvl[:, cs]).then_inc(v_mm, 1)

            for half in range(2):
                values(0, half, half - 1)
            with pe.Fori(1, TILES) as t:
                for half in range(2):
                    values(t, half, t * 2 + half - 1)
            pe.wait_ge(wl_done, 3)
            pe.wait_ge(vl_done, 2 * TILES)

            def project(s, i):
                k, b = where(s)
                wait(pe, hi_done, count(s, 2, i - 1))
                wait(pe, lo_done, count(s, 2, i - 1))
                if i == 0:
                    wait(pe, atl_done, count(s, 1, -4))
                rows = slice(S * b, S * b + S)
                wh, wl = ((wqh, wql), (wkh, wkl))[i]
                three(proj_b[i][:, :], wh[:, k, :], wl[:, k, :], xTh[:, rows], xTl[:, rows]).then_inc(proj_mm, 1)

            def scores_t(m, u):
                idx, r = 5 * m[1] + u, m[1] % 2
                if u == 0:
                    pe.wait_ge(shift_in[r], halfcount(m, 32, 32))
                wait(pe, exp_done, count(m, 5, u - 1))
                for h, j, first in ST[u]:
                    keys, rows = slice(P * j, P * j + P), slice(P * j, S)
                    dst = st_b[idx % 2][:, first:first + S - P * j]
                    st = stack[:, r, h]
                    pe.matmul(dst, st[:, KHI, keys], st[:, QHL, rows], start=True, stop=False)
                    mm = pe.matmul(dst, st[:, KLO, keys], st[:, QSH, rows], start=False, stop=True)
                mm.then_inc(st_mm, 1)

            def scores_n(m, g):
                idx, r = 5 * m[1] + g, m[1] % 2
                if g == 0:
                    pe.wait_ge(dup_done[r], halfcount(m, 96, 96))
                if g == 1:
                    wait(pe, mrow_done, count(m, 1, 0))
                wait(pe, max_done, count(m, 8, ([-2, 0] + SN_CUM)[g]))
                for h, i, first in SN[g]:
                    st = stack[:, r, h]
                    mm = pe.matmul(sn_b[idx % 2][:, first:first + P * (i + 1)], st[:, QHL, P * i:P * i + P],
                                   st[:, KHI, 0:P * (i + 1)], start=True, stop=True)
                mm.then_inc(sn_mm, 1)

            def attend(m, h):
                k, b = where(m)
                pe.wait_ge(pl_done, count(m, 5, 5))
                wait(pe, norm_done, count(m, 2, 0))
                for i in range(QT):
                    dst = o_b[h][:, VW * i:VW * i + VW]
                    for j in range(i + 1):
                        vh = Vh[:, QT * b + j, bass.ds(k * 2 + h, 1), :].rearrange("p a c -> p (a c)")
                        vl = Vl[:, QT * b + j, bass.ds(k * 2 + h, 1), :].rearrange("p a c -> p (a c)")
                        ph, pl = p_block(Ph, m, h, j, i), p_block(Pl, m, h, j, i)
                        pe.matmul(dst, ph, vh, start=(j == 0), stop=False)
                        pe.matmul(dst[:, 0:DH], ph, vl, start=False, stop=False)
                        mm = pe.matmul(dst, pl, vh, start=False, stop=(j == i))
                mm.then_inc(av_mm, 1)

            def step(s):
                m, w, a, t = minus(s, 2), minus(s, 1), minus(s, 3), minus(s, 4)
                if live(s):
                    project(s, 0)
                    project(s, 1)
                if live(m):
                    scores_t(m, 0)
                    scores_t(m, 1)
                if live(w):
                    scores_n(w, 0)
                if live(m):
                    scores_t(m, 2)
                if live(w):
                    scores_n(w, 1)
                if live(t):
                    pe.wait_ge(norm_done, count(t, 2, 2))
                    wait(pe, hi_done, count(s, 2, 1) if live(s) else 2 * STEPS)
                    wait(pe, lo_done, count(s, 2, 1) if live(s) else 2 * STEPS)
                    wait(pe, atl_done, count(t, 1, 0))
                    for q in range(QT):
                        mm = pe.transpose(proj_b[0][:, P * q:P * q + P], An[:, q, :], identf)
                    mm.then_inc(at_mm, 1)
                if live(m):
                    scores_t(m, 3)
                if live(w):
                    scores_n(w, 2)
                if live(m):
                    scores_t(m, 4)
                if live(w):
                    scores_n(w, 3)
                    scores_n(w, 4)
                if live(a):
                    attend(a, 0)
                if live(w):
                    pe.wait_ge(max_done, count(w, 8, 8))
                    pe.transpose(sn_b[(5 * w[1] + 4) % 2][0:8, 0:P], mneg[:, w[1] % 2, :], identf).then_inc(mt_mm, 1)
                if live(a):
                    attend(a, 1)

            pipeline(pe, step)

            pe.wait_ge(w2l_done, 1)
            pe.wait_ge(atl_done, STEPS)
            pe.wait_ge(mrow_done, STEPS)

            def router(b):
                pe.wait_ge(ln2_done, QT * (b + 1))
                wait(pe, x2l_done, b - 1)
                for t in range(QT):
                    mm = pe.transpose(bank[2 + b % 2][:, P * t:P * t + P], xn2[:, QT * b + t, :], identf)
                mm.then_inc(x2t_mm, 1)
                pe.wait_ge(x2l_done, b + 1)
                for t in range(QT * b, QT * b + QT):
                    tok = slice(P * t, P * t + P)
                    three(bank[7][:, E * t:E * t + E], xTh[:, tok], xTl[:, tok], routh, routl).then_inc(rout_mm, 1)

            for b in range(B):
                wait(pe, x1_done, b - 1)
                for t in range(QT):
                    for c in range(PAIRS):
                        tok = slice(P * t, P * t + P)
                        mm = three(bank[b % 2][:, P * t:P * t + P], ATh[:, c, b, tok], ATl[:, c, b, tok],
                                   oh[:, c, :], ol[:, c, :], first=(c == 0), last=(c == PAIRS - 1))
                    mm.then_inc(o_mm, 1)
                if b:
                    router(b - 1)
            router(B - 1)

            def up(n):
                e, b = where(n)
                rows = slice(S * b, S * b + S)
                wait(pe, h_done, count(n, 1, -1))
                for i in range(2):
                    cs = slice(P * i, P * i + P)
                    three(bank[2 * i + n[1] % 2][:, :], uph[:, e, cs], upl[:, e, cs],
                          xTh[:, rows], xTl[:, rows]).then_inc(up_mm, 1)

            def down(m):
                e, b = where(m)
                pe.wait_ge(hl_done, count(m, 1, 1))
                wait(pe, acc_done, count(m, 4, -4))
                for t in range(QT):
                    tok = slice(P * t, P * t + P)
                    mm = three(bank[4 + m[1] % 2][:, tok], hh[:, m[1] % 4, tok], hl[:, m[1] % 4, tok],
                               dnh[:, e, :], dnl[:, e, :])
                mm.then_inc(dn_mm, 1)

            def moe(n):
                if live(n):
                    up(n)
                m = minus(n, 2)
                if live(m):
                    down(m)

            pe.wait_ge(w2l_done, 3)
            pe.wait_ge(x1_done, B)
            pipeline_moe(pe, moe, 2)


_INS = ['L0_attn_x', 'L0_attn_Q_w', 'L0_attn_Q_b', 'L0_attn_K_w', 'L0_attn_K_b', 'L0_attn_V_w', 'L0_attn_V_b',
        'L0_attn_O_w', 'L0_attn_O_b', 'L0_ffn_router_w', 'L0_ffn_up_proj', 'L0_ffn_down_proj']
_OUTS = [((4, 512, 128), 'float32')]


def kernel(**inputs):
    import numpy as _np
    import concourse.bacc as _bacc
    from concourse import mybir as _mybir
    from concourse.bass_utils import run_bass_kernel_spmd as _run

    nc = _bacc.Bacc("TRN2", target_bir_lowering=False, num_devices=1)
    arrays, args = {}, []
    for name in _INS:
        a = _np.ascontiguousarray(inputs[name])
        arrays[f"in_{name}_dram"] = a
        args.append(nc.dram_tensor(f"in_{name}_dram", a.shape, _mybir.dt.from_np(a.dtype), kind="ExternalInput").ap())
    for i, (shape, dtype) in enumerate(_OUTS):
        dt = _mybir.dt.from_np(_np.dtype(dtype))
        args.append(nc.dram_tensor(f"out_{i}_dram", shape, dt, kind="ExternalOutput").ap())
    build(nc, *args)
    r = _run(nc, [arrays], core_ids=[0])
    got = tuple(r.results[0][f"out_{i}_dram"] for i in range(len(_OUTS)))
    return got[0]
```

```python
from contextlib import ExitStack

import concourse.bass as bass
from concourse import mybir

F32 = mybir.dt.float32
F16 = mybir.dt.float16
BF16 = mybir.dt.bfloat16
ALU = mybir.AluOpType
ACT = mybir.ActivationFunctionType
AX_X = mybir.AxisListType.X

P = 128
WS = 16.0
EPS = 1e-5
NEG = -1e30


def build(nc, x, Q_w, Q_b, K_w, K_b, V_w, V_b, O_w, O_b, router_w, up_proj, down_proj, out):
    B, S, D = x.shape
    H, _, DH = Q_w.shape
    E, _, D2 = up_proj.shape
    assert D == P and 2 * DH == P and S == 4 * P and D2 == 2 * P and B == 4
    QT = S // P
    TILES = B * QT
    PAIRS = H // 2
    STEPS = PAIRS * B
    SC = WS * WS * DH ** 0.5
    VW = DH + 1
    VAL, MAX, ROW, EXP, ATT, STORE = 2, 2, 3, 4, 5, 6

    x_t = x.rearrange("b (t p) d -> p (b t) d", p=P)
    out_t = out.rearrange("b (t p) d -> p (b t) d", p=P)

    with ExitStack() as ctx:
        def sem(name):
            return ctx.enter_context(nc.semaphore(name))

        ARENA = 53000
        arena = ctx.enter_context(nc.sbuf_tensor("arena", [P, ARENA], F32))
        at = [0]

        def cut(words):
            a = at[0]
            at[0] += words
            assert at[0] <= ARENA, at[0]
            return a

        def f32(a, *shape):
            n = 1
            for k in shape:
                n *= k
            v = arena[:, a:a + n]
            return v if len(shape) == 1 else v.rearrange(*names(shape), **sizes(shape))

        def f16(a, *shape, dt=F16):
            n = 1
            for k in shape:
                n *= k
            v = arena[:, a:a + (n + 1) // 2].bitcast(dt)[:, 0:n]
            return v if len(shape) == 1 else v.rearrange(*names(shape), **sizes(shape))

        def names(shape):
            ax = "abcdef"[:len(shape)]
            return [f"p ({' '.join(ax)}) -> p {' '.join(ax)}"]

        def sizes(shape):
            return {"abcdef"[i]: k for i, k in enumerate(shape) if i}

        identf = f32(cut(P), P)
        mask = f16(cut(S // 2), S, dt=BF16)
        cols = f32(cut(32), 4, PAIRS)
        routh = f16(cut(E // 2), E)
        routl = f16(cut(E // 2), E)
        stats = f32(cut(TILES * 6), TILES, 6)
        mv = f32(cut(TILES * 2), TILES, 2)
        rstd = f32(cut(TILES), TILES)
        xTh = f16(cut(TILES * P // 2), TILES * P)
        xTl = f16(cut(TILES * P // 2), TILES * P)
        wqh, wql, wkh, wkl, wvh, wvl = (f16(cut(H * DH // 2), PAIRS, P) for _ in range(6))
        Vh = f16(cut(4 * QT * 2 * VW // 2), 4, QT, 2, VW)
        Vl = f16(cut(4 * QT * 2 * DH // 2), 4, QT, 2, DH)
        later_at = cut(8192)
        at_at = cut(PAIRS * TILES * P)
        ATh = f16(at_at, PAIRS, B, S)
        ATl = f16(at_at + PAIRS * TILES * P // 2, PAIRS, B, S)
        stack_at = cut(4 * 2 * 4 * S // 2)
        KLO, KHI, QHL, QSH = range(4)
        stack = f16(stack_at, 4, 4, 2, S)
        src_at = cut(2 * 4 * S // 2)
        halves = f16(src_at, 2, 4, S)
        p32_at = cut(4 * S)
        P32 = f32(p32_at, 4, S)
        ph_at = cut(2 * 2 * 5 * S // 2)
        Ph = f16(ph_at, 2, 5, S)
        Pl = f16(ph_at + 2 * 5 * S // 2, 2, 5, S)
        junk = f16(cut(S), 2, S, dt=BF16)
        mneg = f32(cut(16), 2, 8)
        mrow = f16(cut(P), 2, P)
        rec = f32(cut(8), 8)
        dummy = f32(cut(4), 4)
        bias = f32(cut(4), 3)
        An = f32(cut(S), QT, P)

        xraw = f32(at_at, TILES, P)
        wraw = [f32(at_at + TILES * P + i * H * DH, PAIRS, P) for i in range(3)]
        xn = f32(at_at + TILES * P + 3 * H * DH, TILES, P)
        small = f32(at_at + 2 * TILES * P + 3 * H * DH, P)
        raw2 = f32(later_at, 4 * 1024)
        oraw = raw2[:, 0:PAIRS * P]
        upraw = raw2[:, 1024:1024 + E * D2]
        dnraw = raw2[:, 3072:3072 + E * P]
        w2_at = later_at + 4096
        oh, ol = (f16(w2_at + i * 512, PAIRS, P) for i in range(2))
        uph, upl = (f16(w2_at + 1024 + i * 1024, E, D2) for i in range(2))
        dnh, dnl = (f16(w2_at + 3072 + i * 512, E, P) for i in range(2))
        x1 = f32(stack_at + 4096 + P, TILES, P)
        xn2 = f32(src_at, TILES, P)
        xres = f32(stack_at, TILES, P)
        obb = f32(stack_at + 2048, P)
        xob = f32(stack_at + 2048 + P, TILES, P)
        sil = f32(p32_at, 2, S)
        h32 = f32(p32_at + 2 * S, 2, S)
        hh = f16(ph_at, 4, S)
        hl = f16(ph_at + 4 * S // 2, 4, S)
        gl_at = ph_at + 4 * S
        G = [f32(gl_at + i * TILES * E, TILES, E) for i in range(8)]
        g1 = [f32(gl_at + 8 * TILES * E + i * TILES, TILES) for i in range(4)]
        assert gl_at + 8 * TILES * E + 4 * TILES < at[0] and stack_at + 3 * TILES * P + P <= src_at

        bank = [ctx.enter_context(nc.psum_tensor(f"bank{i}", [P, 512], F32)) for i in range(8)]
        proj_b = bank[0:2]
        st_b = bank[2:4]
        sn_b = bank[4:6]
        o_b = bank[6:8]

        x_in = [sem(f"x_in{b}") for b in range(B)]
        w_in = [sem(f"w_in{i}") for i in range(3)]
        small_in = sem("small_in")
        ident_done, const_done = sem("ident_done"), sem("const_done")
        stat_done, ln_done = sem("stat_done"), sem("ln_done")
        sd_done, rs_done = sem("sd_done"), sem("rs_done")
        xt_mm, xh_done, xl_done = sem("xt_mm"), sem("xh_done"), sem("xl_done")
        cols_mm, cols_done = sem("cols_mm"), sem("cols_done")
        wh_done, wl_done = sem("wh_done"), sem("wl_done")
        v_mm, vh_done, vl_done = sem("v_mm"), sem("vh_done"), sem("vl_done")
        qkbias_done, vbias_done = sem("qkbias_done"), sem("vbias_done")
        proj_mm, hi_done, lo_done = sem("proj_mm"), sem("hi_done"), sem("lo_done")
        dup_done = [sem("dup_done0"), sem("dup_done1")]
        shift_in = [sem("shift_in0"), sem("shift_in1")]
        sn_mm, max_done, mt_mm, mrow_done = sem("sn_mm"), sem("max_done"), sem("mt_mm"), sem("mrow_done")
        st_mm, exp_done, tri_done = sem("st_mm"), sem("exp_done"), sem("tri_done")
        pha_done, phd_done, pl_done = sem("pha_done"), sem("phd_done"), sem("pl_done")
        av_mm, rec_done, norm_done = sem("av_mm"), sem("rec_done"), sem("norm_done")
        at_mm, ath_done, atl_done = sem("at_mm"), sem("ath_done"), sem("atl_done")
        x2_in, w2_in = sem("x2_in"), [sem(f"w2_in{i}") for i in range(3)]
        w2h_done, w2l_done = sem("w2h_done"), sem("w2l_done")
        xob_done = sem("xob_done")
        o_mm, x1_done = sem("o_mm"), sem("x1_done")
        stat2_done, sd2_done, rs2_done, ln2_done = sem("stat2_done"), sem("sd2_done"), sem("rs2_done"), sem("ln2_done")
        x2t_mm, x2h_done, x2l_done = sem("x2t_mm"), sem("x2h_done"), sem("x2l_done")
        rout_mm, chain, gexp_in, gexp_done, gate_done = (
            sem("rout_mm"), sem("chain"), sem("gexp_in"), sem("gexp_done"), sem("gate_done"))
        up_mm, sil_done, h_done, hh_done, hl_done = (
            sem("up_mm"), sem("sil_done"), sem("h_done"), sem("hh_done"), sem("hl_done"))
        dn_mm, acc_done, out_done = sem("dn_mm"), sem("acc_done"), sem("out_done")

        def count(n, per, plus):
            k, c = n
            return k * (B * per) + (per * c + plus)

        def halfcount(n, per, plus):
            k, c = n
            return k * (B // 2 * per) + (per * (c // 2) + plus)

        def wait(eng, s, value):
            if not isinstance(value, int) or value > 0:
                eng.wait_ge(s, value)

        def live(n):
            k, c = n
            return not isinstance(k, int) or 0 <= B * k + c < STEPS

        def minus(n, d):
            return (n[0], n[1] - d)

        def where(n):
            k, c = n
            return k + c // B, c % B

        def pipeline(eng, step):
            for c in range(STORE):
                step((0, c))
            with eng.Fori(1, PAIRS - 1) as k:
                for c in range(STORE - B, STORE):
                    step((k, c))
            for c in range(STORE - B, STORE + B):
                step((PAIRS - 1, c))

        def pipeline_moe(eng, step, lag):
            for c in range(B):
                step((0, c))
            with eng.Fori(1, E) as e:
                for c in range(B):
                    step((e, c))
            for c in range(lag):
                step((E, c))

        SN = [[(0, 3, 0)], [(0, 2, 0), (0, 0, 384)], [(1, 3, 0)], [(1, 2, 0), (1, 0, 384)], [(0, 1, 0), (1, 1, 256)]]
        SN_CUM = [1, 3, 4, 6, 8]
        ST = [[(0, 0, 0)], [(0, 1, 0), (0, 3, 384)], [(1, 0, 0)], [(1, 1, 0), (1, 3, 384)], [(0, 2, 0), (1, 2, 256)]]
        PH_ACT = [0, 1, 2, 4]

        def ph_wait(eng, n, u):
            if u in PH_ACT:
                eng.wait_ge(pha_done, count(n, len(PH_ACT), PH_ACT.index(u) + 1))
            else:
                rest = [w for w in range(5) if w not in PH_ACT]
                eng.wait_ge(phd_done, count(n, len(rest), rest.index(u) + 1))

        def p_block(tile, n, head, j, i):
            for u, parts in enumerate(ST):
                for h, key_tile, first in parts:
                    if h == head and key_tile == j:
                        a = first + (i - j) * P
                        return tile[:, n[1] % 2, u, a:a + P]

        block = ctx.enter_context(nc.Block())

        @block.sync
        def _(sp):
            for b in range(B):
                sp.dma_start(xraw[:, QT * b:QT * b + QT, :], x_t[:, QT * b:QT * b + QT, :]).then_inc(x_in[b], 16)
                if b == 0:
                    sp.dma_start(small[0:8, :], Q_b.rearrange("(a h) d -> a (h d)", h=2)).then_inc(small_in, 16)
                    sp.dma_start(small[8:16, :], K_b.rearrange("(a h) d -> a (h d)", h=2)).then_inc(small_in, 16)
                    sp.dma_start(small[16:24, :], V_b.rearrange("(a h) d -> a (h d)", h=2)).then_inc(small_in, 16)
                    sp.dma_start(small[24:32, :], router_w).then_inc(small_in, 16)
            for i, w in enumerate((Q_w, K_w, V_w)):
                sp.dma_start(wraw[i].rearrange("p a (h d) -> p (a h) d", h=2),
                             w.rearrange("h m d -> m h d")).then_inc(w_in[i], 16)

            def step(s):
                m = minus(s, ROW)
                if live(m):
                    sp.wait_ge(mrow_done, count(m, 1, 1))
                    sp.dma_start(stack[DH:DH + 1, m[1] % 4, QSH, :, :].rearrange("p h (t q) -> p (h t) q", t=QT),
                                 mrow[0:8, m[1] % 2, :]).then_inc(shift_in[m[1] % 2], 16)
                if live(s):
                    r, p = s[1] % 4, s[1] % 2
                    if isinstance(s[0], int):
                        sp.wait_ge(lo_done, count(s, 2, 2))
                    wait(sp, st_mm, count(s, 5, -15))
                    for h in range(2):
                        own = slice(DH * h, DH * h + DH)
                        sp.dma_start(stack[0:DH, r, 0:3, h, :], halves[own, p, 0:3, :]).then_inc(dup_done[p], 16)
                        sp.dma_start(stack[0:DH, r, QSH, h, :], halves[own, p, 2, :]).then_inc(dup_done[p], 16)
                        sp.dma_start(stack[DH:P, r, 1:3, h, :], halves[own, p, 1:4:2, :]).then_inc(dup_done[p], 16)

            sp.wait_ge(const_done, 1)
            pipeline(sp, step)

            sp.wait_ge(av_mm, 2 * STEPS)
            sp.dma_start(oraw.rearrange("p (a m) -> p a m", a=PAIRS),
                         O_w.rearrange("(a h) d m -> (h d) a m", h=2)).then_inc(w2_in[0], 16)
            sp.dma_start(xres[:, :, :], x_t).then_inc(x2_in, 16)
            sp.dma_start(obb[:, :], O_b.rearrange("(a m) -> a m", a=1).broadcast_to([P, D])).then_inc(x2_in, 16)
            sp.dma_start(upraw.rearrange("p (e n) -> p e n", e=E), up_proj.rearrange("e h n -> h e n")).then_inc(w2_in[1], 16)
            sp.dma_start(dnraw.rearrange("p (e n) -> p e n", e=E), down_proj.rearrange("e h n -> h e n")).then_inc(w2_in[2], 16)
            for b in range(B):
                sp.wait_ge(acc_done, 4 * B * (E - 1) + 4 * (b + 1))
                sp.dma_start(out_t[:, QT * b:QT * b + QT, :], x1[:, QT * b:QT * b + QT, :]).then_inc(out_done, 16)
            sp.wait_ge(out_done, 16 * B)

        @block.gpsimd
        def _(pool):
            g = nc.gpsimd
            g.memset(identf, 0.0).then_inc(ident_done, 1)
            pool.wait_ge(ident_done, 1)
            g.affine_select(out=identf, in_=identf, compare_op=ALU.not_equal, fill=1.0, base=0,
                            pattern=[[-1, P]], channel_multiplier=1).then_inc(ident_done, 1)
            pool.wait_ge(ident_done, 2)
            g.memset(mask, 0.0).then_inc(ident_done, 1)
            pool.wait_ge(ident_done, 3)
            g.affine_select(out=mask[:, S - P:S], in_=mask[:, S - P:S], compare_op=ALU.is_ge, fill=NEG, base=0,
                            pattern=[[-1, P]], channel_multiplier=1).then_inc(ident_done, 1)
            pool.wait_ge(ident_done, 4)
            g.memset(dummy, 0.0).then_inc(ident_done, 1)
            pool.wait_ge(ident_done, 5)
            g.memset(Vh[:, :, :, :, DH:VW], 1.0).then_inc(ident_done, 1)
            pool.wait_ge(ident_done, 6)
            for kind in (KLO, QSH):
                for h in range(2):
                    g.memset(stack[DH:P, :, kind, h, :], 0.0).then_inc(ident_done, 1)
            pool.wait_ge(ident_done, 10)
            for h in range(2):
                g.memset(stack[DH:DH + 1, :, KLO, h, :], SC).then_inc(ident_done, 1)
            pool.wait_ge(ident_done, 12)
            g.memset(dummy[:, 1:2], 0.0).then_inc(const_done, 1)
            pool.wait_ge(const_done, 1)

            def low_then_tri(lo, mask_of):
                (n, u), (m, w) = lo, mask_of
                if live(m):
                    pool.wait_ge(exp_done, count(m, 5, w + 1))
                if live(n):
                    if u == 0:
                        wait(pool, av_mm, count(n, 2, -2))
                    ph_wait(pool, n, u)
                    g.tensor_tensor(Pl[:, n[1] % 2, u, :], P32[:, (5 * n[1] + u) % 4, :], Ph[:, n[1] % 2, u, :],
                                    ALU.subtract).then_inc(pl_done, 1)
                if live(m):
                    slot = (5 * m[1] + w) % 4
                    if len(ST[w]) == 1:
                        v, pattern = P32[:, slot, 0:P], [[1, P]]
                    else:
                        a = ST[w][1][2] // P
                        v = P32[:, slot, :].rearrange("p (a q) -> p a q", q=P)[:, 0:a + 1:a, :]
                        pattern = [[0, 2], [1, P]]
                    g.affine_select(out=v, in_=v, compare_op=ALU.is_ge, fill=0.0, base=0, pattern=pattern,
                                    channel_multiplier=-1).then_inc(tri_done, 1)

            def step(s):
                m, n = minus(s, EXP), minus(s, EXP + 1)
                low_then_tri((n, 3), (m, 0))
                low_then_tri((n, 4), (m, 1))
                for u in range(3):
                    low_then_tri((m, u), (m, u + 2))

            pipeline(pool, step)

            pool.wait_ge(x2_in, 32)
            for t in range(TILES):
                g.tensor_tensor(xob[:, t, :], xres[:, t, :], obb[:, :], ALU.add).then_inc(xob_done, 1)

            def moe(n):
                if live(n):
                    pool.wait_ge(hh_done, count(n, 1, 1))
                    wait(pool, dn_mm, count(n, 1, -3))
                    g.tensor_tensor(hl[:, n[1] % 4, :], h32[:, n[1] % 2, :], hh[:, n[1] % 4, :],
                                    ALU.subtract).then_inc(hl_done, 1)

            for c in range(B):
                moe((0, c))
            with pool.Fori(1, E) as e:
                for c in range(B):
                    moe((e, c))

        @block.scalar
        def _(act):
            a = nc.scalar
            for i, dst in enumerate((wqh, wkh, wvh)):
                src = wraw[i].rearrange("p a n -> p (a n)")
                d = dst.rearrange("p a n -> p (a n)")
                if i == 1:
                    act.wait_ge(stat_done, 2 * TILES + 1)
                    a.activation(rstd, rstd, ACT.Sqrt).then_inc(sd_done, 1)
                act.wait_ge(w_in[i], 16)
                a.activation(d, src, ACT.Identity, scale=WS).then_inc(wh_done, 1)
            act.wait_ge(cols_mm, 1)
            a.activation(cols.rearrange("p a n -> p (a n)"), bank[4][:, 0:32], ACT.Identity, scale=WS).then_inc(cols_done, 1)
            act.wait_ge(cols_done, 1)
            a.activation(routh, cols[:, 3, :], ACT.Identity).then_inc(cols_done, 1)
            for b in range(B):
                act.wait_ge(xt_mm, b + 1)
                a.activation(xTh[:, S * b:S * b + S], bank[b][:, :], ACT.Identity).then_inc(xh_done, 1)

            def expo(m, u):
                idx = 5 * m[1] + u
                act.wait_ge(st_mm, count(m, 5, u + 1))
                wait(act, pl_done, count(m, 5, u - 3))
                a.activation(P32[:, idx % 4, :], st_b[idx % 2][:, :], ACT.Exp, scale=1.0 / SC).then_inc(exp_done, 1)

            def high(m, u):
                idx = 5 * m[1] + u
                if u == PH_ACT[0]:
                    wait(act, av_mm, count(m, 2, -2))
                act.wait_ge(tri_done, count(m, 5, u + 1))
                a.activation(Ph[:, m[1] % 2, u, :], P32[:, idx % 4, :], ACT.Identity).then_inc(pha_done, 1)

            def step(s):
                v, w, m, n, t = (minus(s, d) for d in (VAL, ROW, EXP, EXP + 1, STORE))
                if live(w):
                    act.wait_ge(mt_mm, count(w, 1, 1))
                    wait(act, shift_in[w[1] % 2], halfcount(w, 16, 0))
                    a.activation(mrow[0:8, w[1] % 2, :], sn_b[(5 * w[1] + 4) % 2][0:8, 0:P],
                                 ACT.Identity).then_inc(mrow_done, 1)
                if live(s):
                    halves_high(s, 0)
                if live(n):
                    high(n, 4)
                if live(m):
                    expo(m, 0)
                if live(s):
                    halves_high(s, 1)
                if live(m):
                    expo(m, 1)
                if live(v):
                    act.wait_ge(v_mm, count(v, 1, 1))
                    wait(act, av_mm, count(v, 2, -6))
                    a.activation(Vh[:, v[1] % 4, :, :, 0:DH],
                                 proj_b[0][:, :].rearrange("p (t h d) -> p t h d", t=QT, h=2),
                                 ACT.Identity).then_inc(vh_done, 1)
                if live(m):
                    high(m, 0)
                if live(t):
                    k, b = where(t)
                    if b == 0:
                        act.wait_ge(vbias_done, k + 1)
                    act.wait_ge(at_mm, count(t, 1, 1))
                if live(m):
                    expo(m, 2)
                if live(t):
                    a.activation(ATh[:, k, b, :], proj_b[1][:, :], ACT.Identity,
                                 bias=bias[:, 2:3]).then_inc(ath_done, 1)
                if live(m):
                    high(m, 1)
                    expo(m, 3)
                    high(m, 2)
                    expo(m, 4)

            def halves_high(s, i):
                r = s[1] % 2
                if s[1] % B == 0 and i == 0:
                    act.wait_ge(qkbias_done, where(s)[0] + 1)
                act.wait_ge(proj_mm, count(s, 2, i + 1))
                if i == 0:
                    wait(act, dup_done[r], halfcount(s, 96, 0))
                a.activation(halves[:, r, (2, 1)[i], :], proj_b[i][:, :], ACT.Identity,
                             bias=bias[:, i:i + 1]).then_inc(hi_done, 1)

            act.wait_ge(const_done, 1)
            pipeline(act, step)

            for i, (raw, dst) in enumerate(((oraw, oh), (upraw, uph), (dnraw, dnh))):
                act.wait_ge(w2_in[i], 16)
                a.activation(dst.rearrange("p a n -> p (a n)"), raw, ACT.Identity, scale=WS).then_inc(w2h_done, 1)
            for b in range(B):
                act.wait_ge(stat2_done, 9 * (b + 1))
                a.activation(rstd[:, QT * b:QT * b + QT], rstd[:, QT * b:QT * b + QT], ACT.Sqrt).then_inc(sd2_done, 1)
                act.wait_ge(x2t_mm, b + 1)
                a.activation(xTh[:, S * b:S * b + S], bank[2 + b % 2][:, :], ACT.Identity).then_inc(x2h_done, 1)
            act.wait_ge(gexp_in, 1)
            a.activation(G[2], G[1], ACT.Exp).then_inc(gexp_done, 1)

            def silu(n):
                act.wait_ge(up_mm, count(n, 2, 1))
                wait(act, h_done, count(n, 1, -1))
                a.activation(sil[:, n[1] % 2, :], bank[n[1] % 2][:, :], ACT.Silu, scale=1.0 / WS).then_inc(sil_done, 1)

            def hhigh(n):
                act.wait_ge(h_done, count(n, 1, 1))
                wait(act, dn_mm, count(n, 1, -3))
                a.activation(hh[:, n[1] % 4, :], h32[:, n[1] % 2, :], ACT.Identity).then_inc(hh_done, 1)

            def moe(n):
                if live(n):
                    silu(n)
                m = minus(n, 1)
                if live(m):
                    hhigh(m)

            pipeline_moe(act, moe, 1)

        @block.vector
        def _(dve):
            v = nc.vector
            links = [0]

            def link(ins):
                links[0] += 1
                ins.then_inc(chain, 1)
                dve.wait_ge(chain, links[0])

            def layernorm_stats(b, src, done):
                for t in range(QT * b, QT * b + QT):
                    v.bn_stats(stats[:, t, :], src[:, t, :]).then_inc(done, 1)

            for b in range(B):
                dve.wait_ge(x_in[b], 16)
                layernorm_stats(b, xraw, stat_done)
                dve.wait_ge(stat_done, 2 * QT * b + QT)
                for t in range(QT * b, QT * b + QT):
                    v.bn_aggr(mv[:, t, :], stats[:, t, :]).then_inc(stat_done, 1)
            dve.wait_ge(stat_done, 2 * TILES)
            v.tensor_scalar(rstd, mv[:, :, 1], EPS, None, ALU.add).then_inc(stat_done, 1)
            dve.wait_ge(sd_done, 1)
            v.reciprocal(rstd, rstd).then_inc(rs_done, 1)
            dve.wait_ge(rs_done, 1)
            for t in range(TILES):
                v.tensor_scalar(xn[:, t, :], xraw[:, t, :], mv[:, t, 0:1], rstd[:, t:t + 1],
                                ALU.subtract, ALU.mult).then_inc(ln_done, 1)
            for b in range(B):
                dve.wait_ge(xh_done, b + 1)
                v.tensor_tensor(xTl[:, S * b:S * b + S], bank[b][:, :], xTh[:, S * b:S * b + S],
                                ALU.subtract).then_inc(xl_done, 1)
            dve.wait_ge(cols_done, 2)
            v.tensor_tensor(routl, cols[:, 3, :], routh, ALU.subtract).then_inc(cols_done, 1)
            for i, (hi, lo) in enumerate(((wqh, wql), (wkh, wkl), (wvh, wvl))):
                dve.wait_ge(wh_done, 1 + i)
                v.scalar_tensor_tensor(lo.rearrange("p a n -> p (a n)"), wraw[i].rearrange("p a n -> p (a n)"), WS,
                                       hi.rearrange("p a n -> p (a n)"), ALU.mult, ALU.subtract).then_inc(wl_done, 1)

            def maxima(m, g):
                r = m[1] % 2
                if g == 0:
                    wait(dve, mt_mm, count(m, 1, -1))
                dve.wait_ge(sn_mm, count(m, 5, g + 1))
                idx = 5 * m[1] + g
                wait(dve, max_done, count(m, 8, ([0] + SN_CUM)[g]))
                v.memset(dummy[:, 3:4], 0.0)
                for h, i, first in SN[g]:
                    n = P * (i + 1)
                    v.tensor_tensor_reduce(junk[:, idx % 2, first:first + n], sn_b[idx % 2][:, first:first + n],
                                           mask[:, S - n:S], -1.0 / SC, 3e38, ALU.add, ALU.min,
                                           mneg[:, r, QT * h + i:QT * h + i + 1]).then_inc(max_done, 1)

            def high(m, u):
                dve.wait_ge(tri_done, count(m, 5, u + 1))
                if u == min(set(range(5)) - set(PH_ACT)):
                    wait(dve, av_mm, count(m, 2, -2))
                v.tensor_copy(Ph[:, m[1] % 2, u, :], P32[:, (5 * m[1] + u) % 4, :]).then_inc(phd_done, 1)

            def halves_low(s, i):
                hi, lo = ((2, 3), (1, 0))[i]
                r = s[1] % 2
                if i == 0:
                    wait(dve, dup_done[r], halfcount(s, 96, 0))
                dve.wait_ge(hi_done, count(s, 2, i + 1))
                v.scalar_tensor_tensor(halves[:, r, lo, :], proj_b[i][:, :], bias[:, i:i + 1],
                                       halves[:, r, hi, :], ALU.add, ALU.subtract).then_inc(lo_done, 1)

            def step(s):
                vv, w, n, t = minus(s, VAL), minus(s, MAX), minus(s, EXP + 1), minus(s, STORE)
                if live(n):
                    high(n, 3)
                if live(t):
                    dve.wait_ge(av_mm, count(t, 2, 2))
                    wait(dve, norm_done, count(t, 2, 0))
                    k, b = where(t)
                    if b == 0:
                        wait(dve, ath_done, count(t, 1, 0))
                        wait(dve, atl_done, count(t, 1, 0))
                        v.tensor_scalar(bias[:, 2:3], cols[:, 2, bass.ds(k, 1)], 1.0, None,
                                        ALU.mult).then_inc(vbias_done, 1)
                    for h in range(2):
                        v.reciprocal(rec[:, QT * h:QT * h + QT],
                                     o_b[h][:, 0:QT * VW].rearrange("p (t c) -> p t c", t=QT)[:, :, DH]).then_inc(rec_done, 1)
                    dve.wait_ge(rec_done, count(t, 2, 2))
                    wait(dve, at_mm, count(t, 1, 0))
                    for h in range(2):
                        v.tensor_tensor(An[:, :, DH * h:DH * h + DH],
                                        o_b[h][:, 0:QT * VW].rearrange("p (t c) -> p t c", t=QT)[:, :, 0:DH],
                                        rec[:, QT * h:QT * h + QT].unsqueeze(2).broadcast_to([P, QT, DH]),
                                        ALU.mult).then_inc(norm_done, 1)
                if live(s) and s[1] % B == 0:
                    k, _ = where(s)
                    wait(dve, lo_done, count(s, 2, 0))
                    v.tensor_scalar(bias[:, 0:2], cols[:, 0:2, bass.ds(k, 1)].rearrange("p a n -> p (a n)"),
                                    1.0, None, ALU.mult).then_inc(qkbias_done, 1)
                    dve.wait_ge(qkbias_done, k + 1)
                if live(w):
                    maxima(w, 0)
                if live(s):
                    halves_low(s, 0)
                if live(w):
                    maxima(w, 1)
                if live(s):
                    halves_low(s, 1)
                if live(w):
                    maxima(w, 2)
                if live(vv):
                    dve.wait_ge(vh_done, count(vv, 1, 1))
                    v.tensor_tensor(Vl[:, vv[1] % 4, :, :, :],
                                    proj_b[0][:, :].rearrange("p (t h d) -> p t h d", t=QT, h=2),
                                    Vh[:, vv[1] % 4, :, :, 0:DH], ALU.subtract).then_inc(vl_done, 1)
                if live(w):
                    maxima(w, 3)
                if live(t):
                    dve.wait_ge(ath_done, count(t, 1, 1))
                    v.scalar_tensor_tensor(ATl[:, k0(t), t[1] % B, :], proj_b[1][:, :], bias[:, 2:3],
                                           ATh[:, k0(t), t[1] % B, :], ALU.add, ALU.subtract).then_inc(atl_done, 1)
                if live(w):
                    maxima(w, 4)

            def k0(n):
                return where(n)[0]

            dve.wait_ge(const_done, 1)
            pipeline(dve, step)

            for i, (raw, hi, lo) in enumerate(((oraw, oh, ol), (upraw, uph, upl), (dnraw, dnh, dnl))):
                dve.wait_ge(w2h_done, i + 1)
                v.scalar_tensor_tensor(lo.rearrange("p a n -> p (a n)"), raw, WS, hi.rearrange("p a n -> p (a n)"),
                                       ALU.mult, ALU.subtract).then_inc(w2l_done, 1)
            dve.wait_ge(xob_done, TILES)
            for b in range(B):
                tiles = slice(QT * b, QT * b + QT)
                dve.wait_ge(o_mm, QT * (b + 1))
                v.scalar_tensor_tensor(x1[:, tiles, :], bank[b % 2][:, :].rearrange("p (t d) -> p t d", t=QT),
                                       1.0 / (WS * WS), xob[:, tiles, :], ALU.mult, ALU.add).then_inc(x1_done, 1)
                dve.wait_ge(x1_done, b + 1)
                layernorm_stats(b, x1, stat2_done)
                dve.wait_ge(stat2_done, 9 * b + QT)
                for t in range(QT * b, QT * b + QT):
                    v.bn_aggr(mv[:, t, :], stats[:, t, :]).then_inc(stat2_done, 1)
                dve.wait_ge(stat2_done, 9 * b + 2 * QT)
                v.tensor_scalar(rstd[:, tiles], mv[:, tiles, 1], EPS, None, ALU.add).then_inc(stat2_done, 1)
                dve.wait_ge(sd2_done, b + 1)
                v.reciprocal(rstd[:, tiles], rstd[:, tiles]).then_inc(rs2_done, 1)
                dve.wait_ge(rs2_done, b + 1)
                for t in range(QT * b, QT * b + QT):
                    v.tensor_scalar(xn2[:, t, :], x1[:, t, :], mv[:, t, 0:1], rstd[:, t:t + 1],
                                    ALU.subtract, ALU.mult).then_inc(ln2_done, 1)
                dve.wait_ge(x2h_done, b + 1)
                v.tensor_tensor(xTl[:, S * b:S * b + S], bank[2 + b % 2][:, :], xTh[:, S * b:S * b + S],
                                ALU.subtract).then_inc(x2l_done, 1)

            def over_e(t):
                return t.unsqueeze(2).broadcast_to([P, TILES, E])

            dve.wait_ge(rout_mm, TILES)
            link(v.tensor_scalar(G[0], bank[7][:, 0:TILES * E].rearrange("p (t e) -> p t e", e=E),
                                 1.0 / WS, None, ALU.mult))
            for e in range(E):
                v.memset(G[7][:, :, e], float(E - e)).then_inc(chain, 1)
            links[0] += E
            link(v.tensor_reduce(g1[0], G[0], AX_X, ALU.max))
            link(v.tensor_tensor(G[1], G[0], over_e(g1[0]), ALU.subtract))
            v.tensor_copy(G[6], G[1]).then_inc(gexp_in, 1)
            dve.wait_ge(gexp_in, 1)

            def pick(values, onehot):
                link(v.tensor_reduce(g1[1], values, AX_X, ALU.max))
                link(v.tensor_tensor(G[4], values, over_e(g1[1]), ALU.is_ge))
                link(v.tensor_tensor(G[4], G[4], G[7], ALU.mult))
                link(v.tensor_reduce(g1[2], G[4], AX_X, ALU.max))
                link(v.tensor_tensor(onehot, G[4], over_e(g1[2]), ALU.is_ge))

            pick(G[6], G[3])
            link(v.tensor_scalar(G[5], G[3], NEG, None, ALU.mult))
            link(v.tensor_tensor(G[6], G[6], G[5], ALU.add))
            pick(G[6], G[5])
            link(v.tensor_tensor(G[3], G[3], G[5], ALU.add))
            dve.wait_ge(gexp_done, 1)
            link(v.tensor_tensor(G[4], G[2], G[3], ALU.mult))
            link(v.tensor_reduce(g1[1], G[4], AX_X, ALU.add))
            link(v.tensor_scalar(g1[2], g1[1], WS * WS, None, ALU.mult))
            link(v.reciprocal(g1[3], g1[2]))
            v.tensor_tensor(G[0], G[4], over_e(g1[3]), ALU.mult).then_inc(gate_done, 1)
            dve.wait_ge(gate_done, 1)

            def moe(n):
                if live(n):
                    dve.wait_ge(up_mm, count(n, 2, 2))
                    wait(dve, hl_done, count(n, 1, -1))
                    dve.wait_ge(sil_done, count(n, 1, 1))
                    v.tensor_tensor(h32[:, n[1] % 2, :], bank[2 + n[1] % 2][:, :], sil[:, n[1] % 2, :],
                                    ALU.mult).then_inc(h_done, 1)
                m = minus(n, 2)
                if live(m):
                    e, b = where(m)
                    dve.wait_ge(dn_mm, count(m, 1, 1))
                    wait(dve, acc_done, count(m, 4, -8))
                    for t in range(QT):
                        tile = QT * b + t
                        v.scalar_tensor_tensor(x1[:, tile, :], bank[4 + m[1] % 2][:, P * t:P * t + P],
                                               G[0][:, tile, bass.ds(e, 1)], x1[:, tile, :],
                                               ALU.mult, ALU.add).then_inc(acc_done, 1)

            pipeline_moe(dve, moe, 2)

        @block.tensor
        def _(pe):
            def three(dst, ah, al, bh, bl, first=True, last=True):
                pe.matmul(dst, ah, bh, start=first, stop=False)
                pe.matmul(dst, ah, bl, start=False, stop=False)
                return pe.matmul(dst, al, bh, start=False, stop=last)

            pe.wait_ge(small_in, 64)
            pe.wait_ge(ident_done, 2)
            pe.transpose(bank[4][:, 0:32], small[0:32, :], identf[0:32, 0:32]).then_inc(cols_mm, 1)
            for b in range(B):
                pe.wait_ge(ln_done, QT * (b + 1))
                for t in range(QT):
                    mm = pe.transpose(bank[b][:, P * t:P * t + P], xn[:, QT * b + t, :], identf)
                mm.then_inc(xt_mm, 1)

            pe.wait_ge(cols_done, 1)
            pe.wait_ge(xh_done, B)
            pe.wait_ge(xl_done, B)
            pe.wait_ge(wl_done, 3)

            def project(s, i):
                k, b = where(s)
                if i == 0:
                    wait(pe, vl_done, count(s, 1, -VAL))
                else:
                    wait(pe, atl_done, count(s, 1, -STORE))
                if i == 0:
                    wait(pe, lo_done, count(s, 2, -1))
                else:
                    wait(pe, lo_done, count(s, 2, 0))
                rows = slice(S * b, S * b + S)
                wh, wl = ((wqh, wql), (wkh, wkl))[i]
                three(proj_b[i][:, :], wh[:, k, :], wl[:, k, :], xTh[:, rows], xTl[:, rows]).then_inc(proj_mm, 1)

            def values(v):
                k, b = where(v)
                s = (v[0], v[1] + VAL)
                pe.wait_ge(lo_done, count(s, 2, 1) if live(s) else 2 * STEPS)
                wait(pe, vl_done, count(v, 1, 0))
                for t in range(QT):
                    tok = slice(S * b + P * t, S * b + P * t + P)
                    mm = three(proj_b[0][:, P * t:P * t + P], xTh[:, tok], xTl[:, tok], wvh[:, k, :], wvl[:, k, :])
                mm.then_inc(v_mm, 1)

            def scores_t(m, u):
                idx, r = 5 * m[1] + u, m[1] % 4
                if u == 0:
                    pe.wait_ge(shift_in[m[1] % 2], halfcount(m, 16, 16))
                wait(pe, exp_done, count(m, 5, u - 1))
                for h, j, first in ST[u]:
                    keys, rows = slice(P * j, P * j + P), slice(P * j, S)
                    dst = st_b[idx % 2][:, first:first + S - P * j]
                    st = stack[:, r, :, h]
                    pe.matmul(dst, st[:, KHI, keys], st[:, QHL, rows], start=True, stop=False)
                    mm = pe.matmul(dst, st[:, KLO, keys], st[:, QSH, rows], start=False, stop=True)
                mm.then_inc(st_mm, 1)

            def scores_n(m, g):
                idx, r = 5 * m[1] + g, m[1] % 4
                if g == 0:
                    pe.wait_ge(dup_done[m[1] % 2], halfcount(m, 96, 96))
                if g == 1:
                    wait(pe, mrow_done, count(m, 1, 0))
                wait(pe, max_done, count(m, 8, ([-2, 0] + SN_CUM)[g]))
                for h, i, first in SN[g]:
                    st = stack[:, r, :, h]
                    mm = pe.matmul(sn_b[idx % 2][:, first:first + P * (i + 1)], st[:, QHL, P * i:P * i + P],
                                   st[:, KHI, 0:P * (i + 1)], start=True, stop=True)
                mm.then_inc(sn_mm, 1)

            def attend(m, h):
                pe.wait_ge(pl_done, count(m, 5, 5))
                pe.wait_ge(vl_done, count(m, 1, 1))
                wait(pe, norm_done, count(m, 2, 0))
                for i in range(QT):
                    dst = o_b[h][:, VW * i:VW * i + VW]
                    for j in range(i + 1):
                        vh, vl = Vh[:, m[1] % 4, j, h, :], Vl[:, m[1] % 4, j, h, :]
                        ph, pl = p_block(Ph, m, h, j, i), p_block(Pl, m, h, j, i)
                        pe.matmul(dst, ph, vh, start=(j == 0), stop=False)
                        pe.matmul(dst[:, 0:DH], ph, vl, start=False, stop=False)
                        mm = pe.matmul(dst, pl, vh, start=False, stop=(j == i))
                mm.then_inc(av_mm, 1)

            def step(s):
                v, w, x, m, a, t = (minus(s, d) for d in (VAL, MAX, ROW, EXP, ATT, STORE))
                if live(x):
                    pe.wait_ge(max_done, count(x, 8, 8))
                    pe.transpose(sn_b[(5 * x[1] + 4) % 2][0:8, 0:P], mneg[:, x[1] % 2, :], identf).then_inc(mt_mm, 1)
                if live(w):
                    scores_n(w, 0)
                if live(s):
                    project(s, 0)
                if live(m):
                    scores_t(m, 0)
                if live(w):
                    scores_n(w, 1)
                if live(s):
                    project(s, 1)
                if live(m):
                    scores_t(m, 1)
                if live(v):
                    values(v)
                if live(w):
                    scores_n(w, 2)
                if live(m):
                    scores_t(m, 2)
                if live(t):
                    pe.wait_ge(norm_done, count(t, 2, 2))
                    wait(pe, lo_done, count(s, 2, 2) if live(s) else 2 * STEPS)
                    wait(pe, atl_done, count(t, 1, 0))
                    for q in range(QT):
                        mm = pe.transpose(proj_b[1][:, P * q:P * q + P], An[:, q, :], identf)
                    mm.then_inc(at_mm, 1)
                if live(w):
                    scores_n(w, 3)
                if live(m):
                    scores_t(m, 3)
                if live(a):
                    attend(a, 0)
                if live(w):
                    scores_n(w, 4)
                if live(a):
                    attend(a, 1)
                if live(m):
                    scores_t(m, 4)

            pipeline(pe, step)

            pe.wait_ge(w2l_done, 1)
            pe.wait_ge(atl_done, STEPS)
            pe.wait_ge(mrow_done, STEPS)

            def router(b):
                pe.wait_ge(ln2_done, QT * (b + 1))
                wait(pe, x2l_done, b - 1)
                for t in range(QT):
                    mm = pe.transpose(bank[2 + b % 2][:, P * t:P * t + P], xn2[:, QT * b + t, :], identf)
                mm.then_inc(x2t_mm, 1)
                pe.wait_ge(x2l_done, b + 1)
                for t in range(QT * b, QT * b + QT):
                    tok = slice(P * t, P * t + P)
                    three(bank[7][:, E * t:E * t + E], xTh[:, tok], xTl[:, tok], routh, routl).then_inc(rout_mm, 1)

            for b in range(B):
                wait(pe, x1_done, b - 1)
                for t in range(QT):
                    for c in range(PAIRS):
                        tok = slice(P * t, P * t + P)
                        mm = three(bank[b % 2][:, P * t:P * t + P], ATh[:, c, b, tok], ATl[:, c, b, tok],
                                   oh[:, c, :], ol[:, c, :], first=(c == 0), last=(c == PAIRS - 1))
                    mm.then_inc(o_mm, 1)
                if b:
                    router(b - 1)
            router(B - 1)

            def up(n):
                e, b = where(n)
                rows = slice(S * b, S * b + S)
                wait(pe, h_done, count(n, 1, -1))
                for i in range(2):
                    cs = slice(P * i, P * i + P)
                    three(bank[2 * i + n[1] % 2][:, :], uph[:, e, cs], upl[:, e, cs],
                          xTh[:, rows], xTl[:, rows]).then_inc(up_mm, 1)

            def down(m):
                e, b = where(m)
                pe.wait_ge(hl_done, count(m, 1, 1))
                wait(pe, acc_done, count(m, 4, -4))
                for t in range(QT):
                    tok = slice(P * t, P * t + P)
                    mm = three(bank[4 + m[1] % 2][:, tok], hh[:, m[1] % 4, tok], hl[:, m[1] % 4, tok],
                               dnh[:, e, :], dnl[:, e, :])
                mm.then_inc(dn_mm, 1)

            def moe(n):
                if live(n):
                    up(n)
                m = minus(n, 2)
                if live(m):
                    down(m)

            pe.wait_ge(w2l_done, 3)
            pe.wait_ge(x1_done, B)
            pipeline_moe(pe, moe, 2)


_INS = ['L0_attn_x', 'L0_attn_Q_w', 'L0_attn_Q_b', 'L0_attn_K_w', 'L0_attn_K_b', 'L0_attn_V_w', 'L0_attn_V_b',
        'L0_attn_O_w', 'L0_attn_O_b', 'L0_ffn_router_w', 'L0_ffn_up_proj', 'L0_ffn_down_proj']
_OUTS = [((4, 512, 128), 'float32')]


def kernel(**inputs):
    import numpy as _np
    import concourse.bacc as _bacc
    from concourse import mybir as _mybir
    from concourse.bass_utils import run_bass_kernel_spmd as _run

    nc = _bacc.Bacc("TRN2", target_bir_lowering=False, num_devices=1)
    arrays, args = {}, []
    for name in _INS:
        a = _np.ascontiguousarray(inputs[name])
        arrays[f"in_{name}_dram"] = a
        args.append(nc.dram_tensor(f"in_{name}_dram", a.shape, _mybir.dt.from_np(a.dtype), kind="ExternalInput").ap())
    for i, (shape, dtype) in enumerate(_OUTS):
        dt = _mybir.dt.from_np(_np.dtype(dtype))
        args.append(nc.dram_tensor(f"out_{i}_dram", shape, dt, kind="ExternalOutput").ap())
    build(nc, *args)
    r = _run(nc, [arrays], core_ids=[0])
    got = tuple(r.results[0][f"out_{i}_dram"] for i in range(len(_OUTS)))
    return got[0]
```

```python
from contextlib import ExitStack

import concourse.bass as bass
from concourse import mybir

F32 = mybir.dt.float32
F16 = mybir.dt.float16
BF16 = mybir.dt.bfloat16
ALU = mybir.AluOpType
ACT = mybir.ActivationFunctionType
AX_X = mybir.AxisListType.X

P = 128
WS = 16.0
EPS = 1e-5
NEG = -1e30


def build(nc, x, Q_w, Q_b, K_w, K_b, V_w, V_b, O_w, O_b, router_w, up_proj, down_proj, out):
    B, S, D = x.shape
    H, _, DH = Q_w.shape
    E, _, D2 = up_proj.shape
    assert D == P and 2 * DH == P and S == 4 * P and D2 == 2 * P and B == 4
    QT = S // P
    TILES = B * QT
    PAIRS = H // 2
    STEPS = PAIRS * B
    SC = WS * WS * DH ** 0.5
    VW = DH + 1
    VAL, MAX, ROW, EXP, ATT, STORE = 2, 2, 3, 4, 5, 6
    DOWN = 3

    x_t = x.rearrange("b (t p) d -> p (b t) d", p=P)
    out_t = out.rearrange("b (t p) d -> p (b t) d", p=P)

    with ExitStack() as ctx:
        def sem(name):
            return ctx.enter_context(nc.semaphore(name))

        ARENA = 53000
        arena = ctx.enter_context(nc.sbuf_tensor("arena", [P, ARENA], F32))
        at = [0]

        def cut(words):
            a = at[0]
            at[0] += words
            assert at[0] <= ARENA, at[0]
            return a

        def f32(a, *shape):
            n = 1
            for k in shape:
                n *= k
            v = arena[:, a:a + n]
            return v if len(shape) == 1 else v.rearrange(*names(shape), **sizes(shape))

        def f16(a, *shape, dt=F16):
            n = 1
            for k in shape:
                n *= k
            v = arena[:, a:a + (n + 1) // 2].bitcast(dt)[:, 0:n]
            return v if len(shape) == 1 else v.rearrange(*names(shape), **sizes(shape))

        def names(shape):
            ax = "abcdef"[:len(shape)]
            return [f"p ({' '.join(ax)}) -> p {' '.join(ax)}"]

        def sizes(shape):
            return {"abcdef"[i]: k for i, k in enumerate(shape) if i}

        identf = f32(cut(P), P)
        mask = f16(cut(S // 2), S, dt=BF16)
        cols = f32(cut(32), 4, PAIRS)
        routh = f16(cut(E // 2), E)
        routl = f16(cut(E // 2), E)
        stats = f32(cut(TILES * 6), TILES, 6)
        mv = f32(cut(TILES * 2), TILES, 2)
        rstd = f32(cut(TILES), TILES)
        xTh = f16(cut(TILES * P // 2), TILES * P)
        xTl = f16(cut(TILES * P // 2), TILES * P)
        wqh, wql, wkh, wkl, wvh, wvl = (f16(cut(H * DH // 2), PAIRS, P) for _ in range(6))
        Vh = f16(cut(4 * QT * 2 * VW // 2), 4, QT, 2, VW)
        Vl = f16(cut(4 * QT * 2 * DH // 2), 4, QT, 2, DH)
        later_at = cut(8192)
        at_at = cut(PAIRS * TILES * P)
        ATh = f16(at_at, PAIRS, B, S)
        ATl = f16(at_at + PAIRS * TILES * P // 2, PAIRS, B, S)
        stack_at = cut(4 * 2 * 4 * S // 2)
        KLO, KHI, QHL, QSH = range(4)
        stack = f16(stack_at, 4, 4, 2, S)
        src_at = cut(2 * 4 * S // 2)
        halves = f16(src_at, 2, 4, S)
        p32_at = cut(4 * S)
        P32 = f32(p32_at, 4, S)
        ph_at = cut(2 * 2 * 5 * S // 2)
        Ph = f16(ph_at, 2, 5, S)
        Pl = f16(ph_at + 2 * 5 * S // 2, 2, 5, S)
        junk = f16(cut(S), 2, S, dt=BF16)
        mneg = f32(cut(16), 2, 8)
        mrow = f16(cut(P), 2, P)
        rec = f32(cut(8), 8)
        dummy = f32(cut(4), 4)
        bias = f32(cut(4), 3)
        An = f32(cut(S), QT, P)

        xraw = f32(at_at, TILES, P)
        wraw = [f32(at_at + TILES * P + i * H * DH, PAIRS, P) for i in range(3)]
        xn = f32(at_at + TILES * P + 3 * H * DH, TILES, P)
        small = f32(at_at + 2 * TILES * P + 3 * H * DH, P)
        raw2 = f32(later_at, 4 * 1024)
        oraw = raw2[:, 0:PAIRS * P]
        upraw = raw2[:, 1024:1024 + E * D2]
        dnraw = raw2[:, 3072:3072 + E * P]
        w2_at = later_at + 4096
        oh, ol = (f16(w2_at + i * 512, PAIRS, P) for i in range(2))
        uph, upl = (f16(w2_at + 1024 + i * 1024, E, D2) for i in range(2))
        dnh, dnl = (f16(w2_at + 3072 + i * 512, E, P) for i in range(2))
        LATER = [(oraw, oh, ol), (upraw[:, 0:1024], uph[:, 0:E // 2, :], upl[:, 0:E // 2, :]),
                 (upraw[:, 1024:2048], uph[:, E // 2:E, :], upl[:, E // 2:E, :]), (dnraw, dnh, dnl)]
        x1 = f32(stack_at + 2048 + P, TILES, P)
        xn2 = f32(src_at, TILES, P)
        xres = f32(stack_at, TILES, P)
        obb = f32(stack_at + 2048, P)
        sil = f32(p32_at, 2, S)
        h32 = f32(p32_at + 2 * S, 2, S)
        hh = f16(ph_at, 4, S)
        hl = f16(ph_at + 4 * S // 2, 4, S)
        gl_at = ph_at + 4 * S
        G = [f32(gl_at + i * TILES * E, TILES, E) for i in range(8)]
        g1 = [f32(gl_at + 8 * TILES * E + i * TILES, TILES) for i in range(6)]
        assert gl_at + 8 * TILES * E + 6 * TILES < at[0] and stack_at + 2 * TILES * P + P <= src_at

        OUT_BANK = [0, 4, 0, 4]
        ROUT_BANK = [5, 4]
        X2_BANK = [2, 3, 6, 7]
        XT_BANK = [6, 7, 2, 3]
        bank = [ctx.enter_context(nc.psum_tensor(f"bank{i}", [P, 512], F32)) for i in range(8)]
        proj_b = bank[0:2]
        st_b = bank[2:4]
        sn_b = bank[4:6]
        o_b = bank[6:8]

        x_in = [sem(f"x_in{b}") for b in range(B)]
        w_in = [sem(f"w_in{i}") for i in range(3)]
        small_in = sem("small_in")
        ident_done, const_done = sem("ident_done"), sem("const_done")
        stat_done, ln_done = sem("stat_done"), sem("ln_done")
        sd_done, rs_done = sem("sd_done"), sem("rs_done")
        xt_mm, xh_done, xl_done = sem("xt_mm"), sem("xh_done"), sem("xl_done")
        cols_mm, cols_done = sem("cols_mm"), sem("cols_done")
        wh_done, wl_done = sem("wh_done"), sem("wl_done")
        v_mm, vh_done, vl_done = sem("v_mm"), sem("vh_done"), sem("vl_done")
        qkbias_done, vbias_done = sem("qkbias_done"), sem("vbias_done")
        proj_mm, hi_done, lo_done = sem("proj_mm"), sem("hi_done"), sem("lo_done")
        dup_done = [sem("dup_done0"), sem("dup_done1")]
        shift_in = [sem("shift_in0"), sem("shift_in1")]
        sn_mm, max_done, mt_mm, mrow_done = sem("sn_mm"), sem("max_done"), sem("mt_mm"), sem("mrow_done")
        st_mm, exp_done, tri_done = sem("st_mm"), sem("exp_done"), sem("tri_done")
        pha_done, phd_done, pl_done, pld_done = sem("pha_done"), sem("phd_done"), sem("pl_done"), sem("pld_done")
        av_mm, rec_done, norm_done = sem("av_mm"), sem("rec_done"), sem("norm_done")
        at_mm, ath_done, atl_done = sem("at_mm"), sem("ath_done"), sem("atl_done")
        x2_in, w2_in = sem("x2_in"), [sem(f"w2_in{i}") for i in range(4)]
        w2h_done, w2l_done = sem("w2h_done"), sem("w2l_done")
        xob_done = sem("xob_done")
        wrh_done, wrs_done, wrl_done = sem("wrh_done"), sem("wrs_done"), sem("wrl_done")
        o_mm, x1_done = sem("o_mm"), sem("x1_done")
        stat2_done, sd2_done, rs2_done, ln2_done = sem("stat2_done"), sem("sd2_done"), sem("rs2_done"), sem("ln2_done")
        x2t_mm, x2h_done, x2l_done = sem("x2t_mm"), sem("x2h_done"), sem("x2l_done")
        rout_mm, chain, top2_done, tanh_done, gate_done = (
            sem("rout_mm"), sem("chain"), sem("top2_done"), sem("tanh_done"), sem("gate_done"))
        up_mm, sil_done, h_done, hh_done, hl_done = (
            sem("up_mm"), sem("sil_done"), sem("h_done"), sem("hh_done"), sem("hl_done"))
        dn_mm, acc_done, out_done = sem("dn_mm"), sem("acc_done"), sem("out_done")

        def count(n, per, plus):
            k, c = n
            return k * (B * per) + (per * c + plus)

        def halfcount(n, per, plus):
            k, c = n
            return k * (B // 2 * per) + (per * (c // 2) + plus)

        def wait(eng, s, value):
            if not isinstance(value, int) or value > 0:
                eng.wait_ge(s, value)

        def live(n):
            k, c = n
            return not isinstance(k, int) or 0 <= B * k + c < STEPS

        def minus(n, d):
            return (n[0], n[1] - d)

        def number(n):
            k, c = n
            return B * k + c if isinstance(k, int) else -1

        def prev(n):
            k, c = minus(n, 1)
            return (k + c // B, c % B) if isinstance(k, int) else (k, c)

        def where(n):
            k, c = n
            return k + c // B, c % B

        def pipeline(eng, step, between=None):
            for c in range(STORE):
                if between:
                    between(c)
                step((0, c))
            with eng.Fori(1, PAIRS - 1) as k:
                for c in range(STORE - B, STORE):
                    step((k, c))
            for c in range(STORE - B, STORE + B):
                if between:
                    between(B * (PAIRS - 1) + c)
                step((PAIRS - 1, c))

        def pipeline_moe(eng, step, lag, between=None):
            for c in range(B + 1):
                if between:
                    between(c)
                step((0, c))
            with eng.Fori(1, E - 1) as e:
                for c in range(1, B + 1):
                    step((e, c))
            for c in range(1, B + lag):
                step((E - 1, c))

        SN = [[(0, 3, 0)], [(0, 2, 0), (0, 0, 384)], [(1, 3, 0)], [(1, 2, 0), (1, 0, 384)], [(0, 1, 0), (1, 1, 256)]]
        SN_CUM = [1, 3, 4, 6, 8]
        ST = [[(0, 0, 0)], [(0, 1, 0), (0, 3, 384)], [(1, 0, 0)], [(1, 1, 0), (1, 3, 384)], [(0, 2, 0), (1, 2, 256)]]
        PH_ACT = [0, 1, 2, 4]

        def ph_wait(eng, n, u):
            if u in PH_ACT:
                eng.wait_ge(pha_done, count(n, len(PH_ACT), PH_ACT.index(u) + 1))
            else:
                rest = [w for w in range(5) if w not in PH_ACT]
                eng.wait_ge(phd_done, count(n, len(rest), rest.index(u) + 1))

        SHARED = STEPS - B
        PL_DVE = [1, 3]
        PL_POOL = [0, 2, 4]

        def shared(n):
            return number(n) >= SHARED

        def low_wait(eng, n, u):
            if not shared(n):
                wait(eng, pl_done, count(n, 5, u + 1))
            elif u in PL_DVE:
                eng.wait_ge(pld_done, len(PL_DVE) * (number(n) - SHARED) + PL_DVE.index(u) + 1)
            else:
                eng.wait_ge(pl_done, 5 * SHARED + len(PL_POOL) * (number(n) - SHARED) + PL_POOL.index(u) + 1)

        def p_block(tile, n, head, j, i):
            for u, parts in enumerate(ST):
                for h, key_tile, first in parts:
                    if h == head and key_tile == j:
                        a = first + (i - j) * P
                        return tile[:, n[1] % 2, u, a:a + P]

        assert E * B == STEPS

        block = ctx.enter_context(nc.Block())

        @block.sync
        def _(sp):
            def load_x(b):
                sp.dma_start(xraw[:, QT * b:QT * b + QT, :], x_t[:, QT * b:QT * b + QT, :]).then_inc(x_in[b], 16)

            def load_w(i):
                sp.dma_start(wraw[i].rearrange("p a (h d) -> p (a h) d", h=2),
                             (Q_w, K_w, V_w)[i].rearrange("h m d -> m h d")).then_inc(w_in[i], 16)

            load_x(0)
            load_x(1)
            load_w(0)
            sp.dma_start(small[0:8, :], Q_b.rearrange("(a h) d -> a (h d)", h=2)).then_inc(small_in, 16)
            sp.dma_start(small[8:16, :], K_b.rearrange("(a h) d -> a (h d)", h=2)).then_inc(small_in, 16)
            sp.dma_start(small[16:24, :], V_b.rearrange("(a h) d -> a (h d)", h=2)).then_inc(small_in, 16)
            sp.dma_start(small[24:32, :], router_w).then_inc(small_in, 16)
            load_w(1)
            load_x(2)
            load_x(3)
            load_w(2)

            def step(s):
                m = minus(s, ROW)
                if live(m):
                    sp.wait_ge(mrow_done, count(m, 1, 1))
                    sp.dma_start(stack[DH:DH + 1, m[1] % 4, QSH, :, :].rearrange("p h (t q) -> p (h t) q", t=QT),
                                 mrow[0:8, m[1] % 2, :]).then_inc(shift_in[m[1] % 2], 16)
                if live(s):
                    r, p = s[1] % 4, s[1] % 2
                    if isinstance(s[0], int):
                        sp.wait_ge(lo_done, count(s, 2, 2))
                    wait(sp, st_mm, count(s, 5, -15))
                    for h in range(2):
                        own = slice(DH * h, DH * h + DH)
                        sp.dma_start(stack[0:DH, r, 0:3, h, :], halves[own, p, 0:3, :]).then_inc(dup_done[p], 16)
                        sp.dma_start(stack[0:DH, r, QSH, h, :], halves[own, p, 2, :]).then_inc(dup_done[p], 16)
                        sp.dma_start(stack[DH:P, r, 1:3, h, :], halves[own, p, 1:4:2, :]).then_inc(dup_done[p], 16)

            def prepare(c):
                half = slice(E // 2 * (c - 2), E // 2 * (c - 1))
                if c == 1:
                    sp.dma_start(oraw.rearrange("p (a m) -> p a m", a=PAIRS),
                                 O_w.rearrange("(a h) d m -> (h d) a m", h=2)).then_inc(w2_in[0], 16)
                if c in (2, 3):
                    sp.dma_start(upraw.rearrange("p (e n) -> p e n", e=E)[:, half, :],
                                 up_proj[half].rearrange("e h n -> h e n")).then_inc(w2_in[c - 1], 16)
                if c == 4:
                    sp.dma_start(dnraw.rearrange("p (e n) -> p e n", e=E),
                                 down_proj.rearrange("e h n -> h e n")).then_inc(w2_in[3], 16)
                if c == STEPS + 1:
                    sp.wait_ge(st_mm, 5 * (STEPS - 3))
                    sp.dma_start(xres[:, :, :], x_t).then_inc(x2_in, 16)
                if c == STEPS + 2:
                    sp.wait_ge(st_mm, 5 * (STEPS - 2))
                    sp.dma_start(obb[:, :], O_b.rearrange("(a m) -> a m", a=1).broadcast_to([P, D])).then_inc(x2_in, 16)

            sp.wait_ge(const_done, 1)
            pipeline(sp, step, prepare)

            for b in range(B):
                sp.wait_ge(acc_done, 4 * B * (E - 1) + 4 * (b + 1))
                sp.dma_start(out_t[:, QT * b:QT * b + QT, :], x1[:, QT * b:QT * b + QT, :]).then_inc(out_done, 16)
            sp.wait_ge(out_done, 16 * B)

        @block.gpsimd
        def _(pool):
            g = nc.gpsimd
            g.memset(dummy, 0.0).then_inc(ident_done, 1)
            pool.wait_ge(ident_done, 1)
            g.memset(identf, 0.0).then_inc(ident_done, 1)
            pool.wait_ge(ident_done, 2)
            g.affine_select(out=identf, in_=identf, compare_op=ALU.not_equal, fill=1.0, base=0,
                            pattern=[[-1, P]], channel_multiplier=1).then_inc(ident_done, 1)
            pool.wait_ge(ident_done, 3)
            g.memset(mask, 0.0).then_inc(ident_done, 1)
            pool.wait_ge(ident_done, 4)
            g.affine_select(out=mask[:, S - P:S], in_=mask[:, S - P:S], compare_op=ALU.is_ge, fill=NEG, base=0,
                            pattern=[[-1, P]], channel_multiplier=1).then_inc(ident_done, 1)
            pool.wait_ge(ident_done, 5)
            g.memset(Vh[:, :, :, :, DH:VW], 1.0).then_inc(ident_done, 1)
            pool.wait_ge(ident_done, 6)
            for kind in (KLO, QSH):
                g.memset(arena[DH:P, stack_at:stack_at + 8 * 2 * S].rearrange("p (r k n) -> p r k n", r=4, k=4)[:, :, kind, :],
                         0.0).then_inc(ident_done, 1)
            pool.wait_ge(ident_done, 8)
            for h in range(2):
                g.memset(stack[DH:DH + 1, :, KLO, h, :], SC).then_inc(ident_done, 1)
            pool.wait_ge(ident_done, 10)
            g.memset(dummy[:, 1:2], 0.0).then_inc(const_done, 1)
            pool.wait_ge(const_done, 1)

            for i, (hi, lo) in enumerate(((wqh, wql), (wkh, wkl), (wvh, wvl))):
                pool.wait_ge(wrs_done, i + 1)
                g.tensor_tensor(lo[:, 1:PAIRS, :], wraw[i][:, 1:PAIRS, :], hi[:, 1:PAIRS, :],
                                ALU.subtract).then_inc(wrl_done, 1)

            def low_then_tri(lo, mask_of):
                (n, u), (m, w) = lo, mask_of
                if live(m):
                    pool.wait_ge(exp_done, count(m, 5, w + 1))
                if live(n) and not (shared(n) and u in PL_DVE):
                    if u == 0:
                        wait(pool, av_mm, count(n, 2, -2))
                    ph_wait(pool, n, u)
                    g.tensor_tensor(Pl[:, n[1] % 2, u, :], P32[:, (5 * n[1] + u) % 4, :], Ph[:, n[1] % 2, u, :],
                                    ALU.subtract).then_inc(pl_done, 1)
                if live(m):
                    slot = (5 * m[1] + w) % 4
                    if len(ST[w]) == 1:
                        v, pattern = P32[:, slot, 0:P], [[1, P]]
                    else:
                        a = ST[w][1][2] // P
                        v = P32[:, slot, :].rearrange("p (a q) -> p a q", q=P)[:, 0:a + 1:a, :]
                        pattern = [[0, 2], [1, P]]
                    g.affine_select(out=v, in_=v, compare_op=ALU.is_ge, fill=0.0, base=0, pattern=pattern,
                                    channel_multiplier=-1).then_inc(tri_done, 1)

            def step(s):
                m, n = minus(s, EXP), minus(s, EXP + 1)
                low_then_tri((n, 3), (m, 0))
                low_then_tri((n, 4), (m, 1))
                for u in range(3):
                    low_then_tri((m, u), (m, u + 2))

            pipeline(pool, step)

            def moe(n):
                if live(n):
                    pool.wait_ge(hh_done, count(n, 1, 1))
                    wait(pool, dn_mm, count(n, 1, -3))
                    g.tensor_tensor(hl[:, n[1] % 4, :], h32[:, n[1] % 2, :], hh[:, n[1] % 4, :],
                                    ALU.subtract).then_inc(hl_done, 1)

            pipeline_moe(pool, moe, 0)

        @block.scalar
        def _(act):
            a = nc.scalar
            act.wait_ge(ident_done, 1)
            a.activation(dummy[:, 0:1], dummy[:, 0:1], ACT.Sqrt).then_inc(cols_done, 1)

            def weights_high(i):
                act.wait_ge(w_in[i], 16)
                a.activation((wqh, wkh, wvh)[i][:, 0, :], wraw[i][:, 0, :], ACT.Identity, scale=WS).then_inc(wh_done, 1)

            def weights_high_rest(i):
                src = wraw[i][:, 1:PAIRS, :]
                a.activation((wqh, wkh, wvh)[i][:, 1:PAIRS, :], src, ACT.Identity, scale=WS).then_inc(wrh_done, 1)
                act.wait_ge(wrh_done, i + 1)
                a.activation(src, src, ACT.Identity, scale=WS).then_inc(wrs_done, 1)

            def normalise(b, src, dst, ready, done):
                act.wait_ge(ready, 2 * (b + 1))
                for t in range(QT * b, QT * b + QT):
                    a.activation(dst[:, t, :], src[:, t, :], ACT.Identity, bias=mv[:, t, 0:1],
                                 scale=rstd[:, t:t + 1]).then_inc(done, 1)

            def root(b, ready, done):
                act.wait_ge(ready, 9 * (b + 1))
                a.activation(rstd[:, QT * b:QT * b + QT], rstd[:, QT * b:QT * b + QT], ACT.Sqrt).then_inc(done, 1)

            def x_high(b):
                act.wait_ge(xt_mm, b + 1)
                a.activation(xTh[:, S * b:S * b + S], bank[XT_BANK[b]][:, :], ACT.Identity).then_inc(xh_done, 1)

            root(0, stat_done, sd_done)
            x_high(0)
            root(1, stat_done, sd_done)
            weights_high(0)
            act.wait_ge(cols_mm, 1)
            a.activation(cols.rearrange("p a n -> p (a n)"), bank[4][:, 0:32], ACT.Identity, scale=WS).then_inc(cols_done, 1)
            act.wait_ge(cols_done, 2)
            a.activation(routh, cols[:, 3, :], ACT.Identity).then_inc(cols_done, 1)
            weights_high(1)

            def prepare(c):
                if c == 1:
                    root(2, stat_done, sd_done)
                if c == 2:
                    x_high(2)
                    weights_high(2)
                    root(3, stat_done, sd_done)
                    normalise(3, xraw, xn, rs_done, ln_done)
                if c == 3:
                    weights_high_rest(0)
                    weights_high_rest(1)
                if c == 4:
                    weights_high_rest(2)
                if c == STEPS + 5:
                    root(0, stat2_done, sd2_done)
                    normalise(0, x1, xn2, rs2_done, ln2_done)

            def later_high(i):
                raw, dst, _ = LATER[i]
                act.wait_ge(w2_in[i], 16)
                a.activation(dst.rearrange("p a n -> p (a n)"), raw, ACT.Identity, scale=WS).then_inc(w2h_done, 1)

            def expo(m, u):
                idx = 5 * m[1] + u
                act.wait_ge(st_mm, count(m, 5, u + 1))
                if u == 4:
                    low_wait(act, m, 0)
                elif live(minus(m, 1)):
                    low_wait(act, prev(m), u + 1)
                a.activation(P32[:, idx % 4, :], st_b[idx % 2][:, :], ACT.Exp, scale=1.0 / SC).then_inc(exp_done, 1)

            def high(m, u):
                idx = 5 * m[1] + u
                if u == PH_ACT[0]:
                    wait(act, av_mm, count(m, 2, -2))
                act.wait_ge(tri_done, count(m, 5, u + 1))
                a.activation(Ph[:, m[1] % 2, u, :], P32[:, idx % 4, :], ACT.Identity).then_inc(pha_done, 1)

            def step(s):
                v, w, m, n, t = (minus(s, d) for d in (VAL, ROW, EXP, EXP + 1, STORE))
                if live(w):
                    act.wait_ge(mt_mm, count(w, 1, 1))
                    wait(act, shift_in[w[1] % 2], halfcount(w, 16, 0))
                    a.activation(mrow[0:8, w[1] % 2, :], sn_b[(5 * w[1] + 4) % 2][0:8, 0:P],
                                 ACT.Identity).then_inc(mrow_done, 1)
                if live(s):
                    halves_high(s, 0)
                if number(s) in (0, 2):
                    x_high(number(s) + 1)
                if number(s) == 1:
                    normalise(2, xraw, xn, rs_done, ln_done)
                if live(m):
                    expo(m, 0)
                if live(s):
                    halves_high(s, 1)
                if live(n):
                    high(n, 4)
                if live(m):
                    expo(m, 1)
                if STEPS < number(s) <= STEPS + 4:
                    later_high(number(s) - STEPS - 1)
                if live(v):
                    act.wait_ge(v_mm, count(v, 1, 1))
                    wait(act, av_mm, count(v, 2, -6))
                    a.activation(Vh[:, v[1] % 4, :, :, 0:DH],
                                 proj_b[0][:, :].rearrange("p (t h d) -> p t h d", t=QT, h=2),
                                 ACT.Identity).then_inc(vh_done, 1)
                if live(m):
                    high(m, 0)
                if live(t):
                    k, b = where(t)
                    if b == 0:
                        act.wait_ge(vbias_done, k + 1)
                    act.wait_ge(at_mm, count(t, 1, 1))
                if live(m):
                    expo(m, 2)
                if live(t):
                    a.activation(ATh[:, k, b, :], proj_b[1][:, :], ACT.Identity,
                                 bias=bias[:, 2:3]).then_inc(ath_done, 1)
                if live(m):
                    high(m, 1)
                    expo(m, 3)
                    high(m, 2)
                    expo(m, 4)

            def halves_high(s, i):
                r = s[1] % 2
                if s[1] % B == 0 and i == 0:
                    act.wait_ge(qkbias_done, where(s)[0] + 1)
                act.wait_ge(proj_mm, count(s, 2, i + 1))
                if i == 0:
                    wait(act, dup_done[r], halfcount(s, 96, 0))
                a.activation(halves[:, r, (2, 1)[i], :], proj_b[i][:, :], ACT.Identity,
                             bias=bias[:, i:i + 1]).then_inc(hi_done, 1)

            act.wait_ge(const_done, 1)
            pipeline(act, step, prepare)

            def x2_high(b):
                act.wait_ge(x2t_mm, b + 1)
                a.activation(xTh[:, S * b:S * b + S], bank[X2_BANK[b]][:, :], ACT.Identity).then_inc(x2h_done, 1)

            def gate_tanh(i):
                tiles = slice(TILES // 2 * i, TILES // 2 * i + TILES // 2)
                act.wait_ge(top2_done, i + 1)
                a.activation(g1[3][:, tiles], g1[1][:, tiles], ACT.Tanh, scale=0.5 / WS).then_inc(tanh_done, 1)

            root(1, stat2_done, sd2_done)
            normalise(1, x1, xn2, rs2_done, ln2_done)
            x2_high(0)
            x2_high(1)
            root(2, stat2_done, sd2_done)
            x2_high(2)
            root(3, stat2_done, sd2_done)

            def silu(n):
                act.wait_ge(up_mm, count(n, 2, 1))
                wait(act, h_done, count(n, 1, -1))
                a.activation(sil[:, n[1] % 2, :], bank[n[1] % 2][:, :], ACT.Silu, scale=1.0 / WS).then_inc(sil_done, 1)

            def hhigh(n):
                act.wait_ge(h_done, count(n, 1, 1))
                wait(act, dn_mm, count(n, 1, -3))
                a.activation(hh[:, n[1] % 4, :], h32[:, n[1] % 2, :], ACT.Identity).then_inc(hh_done, 1)

            def moe(n):
                if live(n):
                    silu(n)
                if number(n) == 1:
                    x2_high(B - 1)
                if number(n) == 2:
                    gate_tanh(0)
                m = minus(n, 1)
                if live(m):
                    hhigh(m)
                if number(n) == 4:
                    gate_tanh(1)

            pipeline_moe(act, moe, 1)

        @block.vector
        def _(dve):
            v = nc.vector
            links = [0]

            def link(ins):
                links[0] += 1
                ins.then_inc(chain, 1)
                dve.wait_ge(chain, links[0])

            def statistics(b, src, done):
                for t in range(QT * b, QT * b + QT):
                    v.bn_stats(stats[:, t, :], src[:, t, :]).then_inc(done, 1)
                dve.wait_ge(done, 9 * b + QT)
                for t in range(QT * b, QT * b + QT):
                    v.bn_aggr(mv[:, t, :], stats[:, t, :]).then_inc(done, 1)
                dve.wait_ge(done, 9 * b + 2 * QT)
                v.tensor_scalar(rstd[:, QT * b:QT * b + QT], mv[:, QT * b:QT * b + QT, 1], EPS, None,
                                ALU.add).then_inc(done, 1)

            def inverse(b, root_done, done):
                tiles = slice(QT * b, QT * b + QT)
                dve.wait_ge(root_done, b + 1)
                v.reciprocal(rstd[:, tiles], rstd[:, tiles]).then_inc(done, 1)
                dve.wait_ge(done, 2 * b + 1)
                v.scalar_tensor_tensor(mv[:, tiles, 0], mv[:, tiles, 0], -1.0, rstd[:, tiles],
                                       ALU.mult, ALU.mult).then_inc(done, 1)

            def normalise(b, src, dst, root_done, inverse_done, done):
                tiles = slice(QT * b, QT * b + QT)
                dve.wait_ge(root_done, b + 1)
                v.reciprocal(rstd[:, tiles], rstd[:, tiles]).then_inc(inverse_done, 2)
                dve.wait_ge(inverse_done, 2 * (b + 1))
                for t in range(QT * b, QT * b + QT):
                    v.tensor_scalar(dst[:, t, :], src[:, t, :], mv[:, t, 0:1], rstd[:, t:t + 1],
                                    ALU.subtract, ALU.mult).then_inc(done, 1)

            def x_low(b):
                dve.wait_ge(xh_done, b + 1)
                v.tensor_tensor(xTl[:, S * b:S * b + S], bank[XT_BANK[b]][:, :], xTh[:, S * b:S * b + S],
                                ALU.subtract).then_inc(xl_done, 1)

            def weights_low(i):
                hi, lo = ((wqh, wql), (wkh, wkl), (wvh, wvl))[i]
                dve.wait_ge(wh_done, 1 + i)
                v.scalar_tensor_tensor(lo[:, 0, :], wraw[i][:, 0, :], WS, hi[:, 0, :],
                                       ALU.mult, ALU.subtract).then_inc(wl_done, 1)

            dve.wait_ge(x_in[0], 16)
            statistics(0, xraw, stat_done)
            normalise(0, xraw, xn, sd_done, rs_done, ln_done)
            dve.wait_ge(x_in[1], 16)
            statistics(1, xraw, stat_done)
            x_low(0)
            weights_low(0)
            normalise(1, xraw, xn, sd_done, rs_done, ln_done)
            weights_low(1)
            dve.wait_ge(cols_done, 3)
            v.tensor_tensor(routl, cols[:, 3, :], routh, ALU.subtract).then_inc(cols_done, 1)

            def prepare(c):
                if c == 1:
                    inverse(2, sd_done, rs_done)
                if c == 2:
                    x_low(2)
                    weights_low(2)
                    inverse(3, sd_done, rs_done)
                if c == STEPS + 5:
                    residual(0)
                    inverse(0, sd2_done, rs2_done)

            def later_low(i):
                raw, hi, lo = LATER[i]
                dve.wait_ge(w2h_done, i + 1)
                v.scalar_tensor_tensor(lo.rearrange("p a n -> p (a n)"), raw, WS, hi.rearrange("p a n -> p (a n)"),
                                       ALU.mult, ALU.subtract).then_inc(w2l_done, 1)

            def fill(s):
                c = number(s)
                if c == STEPS + 2:
                    later_low(0)
                    later_low(1)
                if c == STEPS + 4:
                    later_low(2)
                if c == STEPS + 3:
                    dve.wait_ge(x2_in, 32)
                    v.tensor_tensor(xres, xres, obb.unsqueeze(1).broadcast_to([P, TILES, P]), ALU.add).then_inc(xob_done, 1)
                if c == STEPS + 5:
                    residual(1)

            def low(n, u):
                if u in PH_ACT:
                    ph_wait(dve, n, u)
                v.tensor_tensor(Pl[:, n[1] % 2, u, :], P32[:, (5 * n[1] + u) % 4, :], Ph[:, n[1] % 2, u, :],
                                ALU.subtract).then_inc(pld_done, 1)

            def residual(b):
                tiles = slice(QT * b, QT * b + QT)
                dve.wait_ge(o_mm, QT * (b + 1))
                if b == 0:
                    dve.wait_ge(xob_done, 1)
                v.scalar_tensor_tensor(x1[:, tiles, :], bank[OUT_BANK[b]][:, :].rearrange("p (t d) -> p t d", t=QT),
                                       1.0 / (WS * WS), xres[:, tiles, :], ALU.mult, ALU.add).then_inc(x1_done, 1)
                dve.wait_ge(x1_done, b + 1)
                statistics(b, x1, stat2_done)

            def maxima(m, g):
                r = m[1] % 2
                if g == 0:
                    wait(dve, mt_mm, count(m, 1, -1))
                dve.wait_ge(sn_mm, count(m, 5, g + 1))
                idx = 5 * m[1] + g
                wait(dve, max_done, count(m, 8, ([0] + SN_CUM)[g]))
                v.memset(dummy[:, 3:4], 0.0)
                for h, i, first in SN[g]:
                    n = P * (i + 1)
                    v.tensor_tensor_reduce(junk[:, idx % 2, first:first + n], sn_b[idx % 2][:, first:first + n],
                                           mask[:, S - n:S], -1.0 / SC, 3e38, ALU.add, ALU.min,
                                           mneg[:, r, QT * h + i:QT * h + i + 1]).then_inc(max_done, 1)

            def high(m, u):
                dve.wait_ge(tri_done, count(m, 5, u + 1))
                if u == min(set(range(5)) - set(PH_ACT)):
                    wait(dve, av_mm, count(m, 2, -2))
                v.tensor_copy(Ph[:, m[1] % 2, u, :], P32[:, (5 * m[1] + u) % 4, :]).then_inc(phd_done, 1)

            def halves_low(s, i):
                hi, lo = ((2, 3), (1, 0))[i]
                r = s[1] % 2
                if i == 0:
                    wait(dve, dup_done[r], halfcount(s, 96, 0))
                dve.wait_ge(hi_done, count(s, 2, i + 1))
                v.scalar_tensor_tensor(halves[:, r, lo, :], proj_b[i][:, :], bias[:, i:i + 1],
                                       halves[:, r, hi, :], ALU.add, ALU.subtract).then_inc(lo_done, 1)

            def step(s):
                vv, w, m, n, t = (minus(s, d) for d in (VAL, MAX, EXP, EXP + 1, STORE))
                if live(t):
                    dve.wait_ge(av_mm, count(t, 2, 2))
                    wait(dve, norm_done, count(t, 2, 0))
                    k, b = where(t)
                    if b == 0:
                        wait(dve, ath_done, count(t, 1, 0))
                        wait(dve, atl_done, count(t, 1, 0))
                        v.tensor_scalar(bias[:, 2:3], cols[:, 2, bass.ds(k, 1)], 1.0, None,
                                        ALU.mult).then_inc(vbias_done, 1)
                    for h in range(2):
                        v.reciprocal(rec[:, QT * h:QT * h + QT],
                                     o_b[h][:, 0:QT * VW].rearrange("p (t c) -> p t c", t=QT)[:, :, DH]).then_inc(rec_done, 1)
                    wait(dve, at_mm, count(t, 1, 0))
                    for h in range(2):
                        dve.wait_ge(rec_done, count(t, 2, h + 1))
                        v.tensor_tensor(An[:, :, DH * h:DH * h + DH],
                                        o_b[h][:, 0:QT * VW].rearrange("p (t c) -> p t c", t=QT)[:, :, 0:DH],
                                        rec[:, QT * h:QT * h + QT].unsqueeze(2).broadcast_to([P, QT, DH]),
                                        ALU.mult).then_inc(norm_done, 1)
                if live(n):
                    high(n, 3)
                    if shared(n):
                        dve.wait_ge(phd_done, count(n, 1, 1))
                        low(n, 3)
                fill(s)
                if live(s) and s[1] % B == 0:
                    k, _ = where(s)
                    wait(dve, lo_done, count(s, 2, 0))
                    v.tensor_scalar(bias[:, 0:2], cols[:, 0:2, bass.ds(k, 1)].rearrange("p a n -> p (a n)"),
                                    1.0, None, ALU.mult).then_inc(qkbias_done, 1)
                    dve.wait_ge(qkbias_done, k + 1)
                if live(w):
                    maxima(w, 0)
                if live(s):
                    halves_low(s, 0)
                    if number(s) in (0, 2):
                        x_low(number(s) + 1)
                    if number(s) in (0, 1):
                        dve.wait_ge(x_in[number(s) + 2], 16)
                        statistics(number(s) + 2, xraw, stat_done)
                if live(w):
                    maxima(w, 1)
                if live(s):
                    halves_low(s, 1)
                if live(w):
                    maxima(w, 2)
                if live(vv):
                    dve.wait_ge(vh_done, count(vv, 1, 1))
                    v.tensor_tensor(Vl[:, vv[1] % 4, :, :, :],
                                    proj_b[0][:, :].rearrange("p (t h d) -> p t h d", t=QT, h=2),
                                    Vh[:, vv[1] % 4, :, :, 0:DH], ALU.subtract).then_inc(vl_done, 1)
                if live(w):
                    maxima(w, 3)
                if live(t):
                    dve.wait_ge(ath_done, count(t, 1, 1))
                    v.scalar_tensor_tensor(ATl[:, k0(t), t[1] % B, :], proj_b[1][:, :], bias[:, 2:3],
                                           ATh[:, k0(t), t[1] % B, :], ALU.add, ALU.subtract).then_inc(atl_done, 1)
                if live(m) and shared(m):
                    low(m, 1)
                if live(w):
                    maxima(w, 4)

            def k0(n):
                return where(n)[0]

            dve.wait_ge(const_done, 1)
            pipeline(dve, step, prepare)

            def x2_low(b):
                dve.wait_ge(x2h_done, b + 1)
                v.tensor_tensor(xTl[:, S * b:S * b + S], bank[X2_BANK[b]][:, :], xTh[:, S * b:S * b + S],
                                ALU.subtract).then_inc(x2l_done, 1)

            def gates(i, meanwhile=None):
                n = TILES // 2
                tiles = slice(n * i, n * i + n)
                first, cand, second, rest, order, shifted = (t[:, tiles, :] for t in (G[1], G[2], G[3], G[4], G[7], G[5]))
                top, top2, best, th, w1, w2 = (t[:, tiles] for t in g1)
                logit = bank[ROUT_BANK[i]][:, 0:E * n].rearrange("p (t e) -> p t e", e=E)

                def over_e(t):
                    return t.unsqueeze(2).broadcast_to([P, n, E])

                dve.wait_ge(rout_mm, n * (i + 1))
                link(v.tensor_reduce(top, logit, AX_X, ALU.max))
                link(v.tensor_tensor(shifted, logit, over_e(top), ALU.subtract))
                link(v.scalar_tensor_tensor(cand, shifted, 0.0, order, ALU.is_ge, ALU.mult))
                link(v.tensor_reduce(best, cand, AX_X, ALU.max))
                link(v.tensor_tensor(first, cand, over_e(best), ALU.is_ge))
                link(v.scalar_tensor_tensor(rest, first, NEG, shifted, ALU.mult, ALU.add))
                v.tensor_reduce(top2, rest, AX_X, ALU.max).then_inc(top2_done, 1)
                if meanwhile:
                    meanwhile()
                dve.wait_ge(top2_done, i + 1)
                link(v.tensor_tensor(cand, rest, over_e(top2), ALU.is_ge))
                link(v.tensor_tensor(cand, cand, order, ALU.mult))
                link(v.tensor_reduce(best, cand, AX_X, ALU.max))
                v.tensor_tensor(second, cand, over_e(best), ALU.is_ge).then_inc(chain, 1)
                c = 0.5 / (WS * WS)
                dve.wait_ge(tanh_done, i + 1)
                v.tensor_scalar(w1, th, -c, c, ALU.mult, ALU.add).then_inc(chain, 1)
                links[0] += 2
                link(v.tensor_scalar(w2, th, c, c, ALU.mult, ALU.add))
                v.tensor_tensor(first, first, over_e(w1), ALU.mult).then_inc(chain, 1)
                links[0] += 1
                link(v.tensor_tensor(second, second, over_e(w2), ALU.mult))
                v.tensor_tensor(G[0][:, tiles, :], first, second, ALU.add).then_inc(gate_done, 1)

            for e in range(E):
                v.memset(G[7][:, :, e], float(E - e)).then_inc(chain, 1)
            links[0] += E
            inverse(1, sd2_done, rs2_done)
            later_low(3)
            x2_low(0)
            residual(2)
            x2_low(1)
            normalise(2, x1, xn2, sd2_done, rs2_done, ln2_done)
            x2_low(2)
            residual(3)
            normalise(3, x1, xn2, sd2_done, rs2_done, ln2_done)
            dve.wait_ge(chain, links[0])

            def prepare2(c):
                if c == 4:
                    gates(1, lambda: moe((1, 0)))
                    dve.wait_ge(gate_done, 2)

            def moe(n):
                if live(n):
                    dve.wait_ge(up_mm, count(n, 2, 2))
                    wait(dve, hl_done, count(n, 1, -1))
                    dve.wait_ge(sil_done, count(n, 1, 1))
                    v.tensor_tensor(h32[:, n[1] % 2, :], bank[2 + n[1] % 2][:, :], sil[:, n[1] % 2, :],
                                    ALU.mult).then_inc(h_done, 1)
                m = minus(n, DOWN)
                if live(m):
                    e, b = where(m)
                    dve.wait_ge(dn_mm, count(m, 1, 1))
                    wait(dve, acc_done, count(m, 4, 0))
                    for t in range(QT):
                        tile = QT * b + t
                        v.scalar_tensor_tensor(x1[:, tile, :], bank[6 + m[1] % 2][:, P * t:P * t + P],
                                               G[0][:, tile, bass.ds(e, 1)], x1[:, tile, :],
                                               ALU.mult, ALU.add).then_inc(acc_done, 1)

            def others(n):
                if number(n) == 3:
                    dve.wait_ge(gate_done, 1)
                if number(n) not in (0, 1, 2, 4):
                    moe(n)

            moe((0, 0))
            moe((0, 1))
            x2_low(B - 1)
            gates(0, lambda: moe((0, 2)))
            pipeline_moe(dve, others, DOWN, prepare2)

        @block.tensor
        def _(pe):
            def three(dst, ah, al, bh, bl, first=True, last=True):
                pe.matmul(dst, ah, bh, start=first, stop=False)
                pe.matmul(dst, ah, bl, start=False, stop=False)
                return pe.matmul(dst, al, bh, start=False, stop=last)

            def x_transposed(b):
                pe.wait_ge(ln_done, QT * (b + 1))
                for t in range(QT):
                    mm = pe.transpose(bank[XT_BANK[b]][:, P * t:P * t + P], xn[:, QT * b + t, :], identf)
                mm.then_inc(xt_mm, 1)

            pe.wait_ge(ident_done, 3)
            x_transposed(0)
            pe.wait_ge(small_in, 64)
            pe.transpose(bank[4][:, 0:32], small[0:32, :], identf[0:32, 0:32]).then_inc(cols_mm, 1)

            def prepare(c):
                if c == 2:
                    pe.wait_ge(cols_done, 2)
                if c == 4:
                    pe.wait_ge(wrl_done, 2)
                if c == 2:
                    x_transposed(2)

            def x2_transposed(b):
                pe.wait_ge(ln2_done, QT * (b + 1))
                for t in range(QT):
                    mm = pe.transpose(bank[X2_BANK[b]][:, P * t:P * t + P], xn2[:, QT * b + t, :], identf)
                mm.then_inc(x2t_mm, 1)

            def project_out(s, t):
                b = number(s) - (STEPS + STORE - B + 1)
                if b < 0:
                    return
                if t == 0:
                    pe.wait_ge(w2l_done, 1)
                    pe.wait_ge(atl_done, STEPS - B + b + 1)
                    wait(pe, x1_done, b - 1)
                for c in range(PAIRS):
                    tok = slice(P * t, P * t + P)
                    mm = three(bank[OUT_BANK[b]][:, P * t:P * t + P], ATh[:, c, b, tok], ATl[:, c, b, tok],
                               oh[:, c, :], ol[:, c, :], first=(c == 0), last=(c == PAIRS - 1))
                mm.then_inc(o_mm, 1)

            def project(s, i):
                k, b = where(s)
                if i == 0:
                    wait(pe, vl_done, count(s, 1, -VAL))
                else:
                    wait(pe, atl_done, count(s, 1, -STORE))
                if i == 0:
                    wait(pe, lo_done, count(s, 2, -1))
                else:
                    wait(pe, lo_done, count(s, 2, 0))
                if isinstance(s[0], int) and s[0] == 0:
                    pe.wait_ge(xl_done, b + 1)
                    pe.wait_ge(wl_done, i + 1)
                rows = slice(S * b, S * b + S)
                wh, wl = ((wqh, wql), (wkh, wkl))[i]
                three(proj_b[i][:, :], wh[:, k, :], wl[:, k, :], xTh[:, rows], xTl[:, rows]).then_inc(proj_mm, 1)

            def values(v):
                k, b = where(v)
                s = (v[0], v[1] + VAL)
                pe.wait_ge(lo_done, count(s, 2, 1) if live(s) else 2 * STEPS)
                wait(pe, vl_done, count(v, 1, 0))
                if number(v) == B:
                    pe.wait_ge(wrl_done, 3)
                if number(v) == 0:
                    pe.wait_ge(wl_done, 3)
                for t in range(QT):
                    tok = slice(S * b + P * t, S * b + P * t + P)
                    mm = three(proj_b[0][:, P * t:P * t + P], xTh[:, tok], xTl[:, tok], wvh[:, k, :], wvl[:, k, :])
                mm.then_inc(v_mm, 1)

            def scores_t(m, u):
                idx, r = 5 * m[1] + u, m[1] % 4
                if u == 0:
                    pe.wait_ge(shift_in[m[1] % 2], halfcount(m, 16, 16))
                wait(pe, exp_done, count(m, 5, u - 1))
                for h, j, first in ST[u]:
                    keys, rows = slice(P * j, P * j + P), slice(P * j, S)
                    dst = st_b[idx % 2][:, first:first + S - P * j]
                    st = stack[:, r, :, h]
                    pe.matmul(dst, st[:, KHI, keys], st[:, QHL, rows], start=True, stop=False)
                    mm = pe.matmul(dst, st[:, KLO, keys], st[:, QSH, rows], start=False, stop=True)
                mm.then_inc(st_mm, 1)

            def scores_n(m, g):
                idx, r = 5 * m[1] + g, m[1] % 4
                if g == 0:
                    pe.wait_ge(dup_done[m[1] % 2], halfcount(m, 96, 96))
                if g == 1:
                    wait(pe, mrow_done, count(m, 1, 0))
                wait(pe, max_done, count(m, 8, ([-2, 0] + SN_CUM)[g]))
                for h, i, first in SN[g]:
                    st = stack[:, r, :, h]
                    mm = pe.matmul(sn_b[idx % 2][:, first:first + P * (i + 1)], st[:, QHL, P * i:P * i + P],
                                   st[:, KHI, 0:P * (i + 1)], start=True, stop=True)
                mm.then_inc(sn_mm, 1)

            def attend(m, h):
                for u in (PL_DVE[-1:] if shared(m) else []) + [4]:
                    low_wait(pe, m, u)
                pe.wait_ge(vl_done, count(m, 1, 1))
                wait(pe, norm_done, count(m, 2, 0))
                for i in range(QT):
                    dst = o_b[h][:, VW * i:VW * i + VW]
                    for j in range(i + 1):
                        vh, vl = Vh[:, m[1] % 4, j, h, :], Vl[:, m[1] % 4, j, h, :]
                        ph, pl = p_block(Ph, m, h, j, i), p_block(Pl, m, h, j, i)
                        pe.matmul(dst, ph, vh, start=(j == 0), stop=False)
                        pe.matmul(dst[:, 0:DH], ph, vl, start=False, stop=False)
                        mm = pe.matmul(dst, pl, vh, start=False, stop=(j == i))
                mm.then_inc(av_mm, 1)

            def step(s):
                v, w, x, m, a, t = (minus(s, d) for d in (VAL, MAX, ROW, EXP, ATT, STORE))
                if number(s) == 2:
                    project(s, 0)
                if live(w):
                    scores_n(w, 0)
                if live(x):
                    pe.wait_ge(max_done, count(x, 8, 8))
                    pe.transpose(sn_b[(5 * x[1] + 4) % 2][0:8, 0:P], mneg[:, x[1] % 2, :], identf).then_inc(mt_mm, 1)
                if live(s) and number(s) != 2:
                    project(s, 0)
                if live(m):
                    scores_t(m, 0)
                if number(s) in (0, 2):
                    x_transposed(number(s) + 1)
                if live(s):
                    project(s, 1)
                if live(w):
                    scores_n(w, 1)
                if live(m):
                    scores_t(m, 1)
                project_out(s, 0)
                if live(v):
                    values(v)
                if live(w):
                    scores_n(w, 2)
                if live(m):
                    scores_t(m, 2)
                if live(t):
                    pe.wait_ge(norm_done, count(t, 2, 2))
                    wait(pe, lo_done, count(s, 2, 2) if live(s) else 2 * STEPS)
                    wait(pe, atl_done, count(t, 1, 0))
                    for q in range(QT):
                        mm = pe.transpose(proj_b[1][:, P * q:P * q + P], An[:, q, :], identf)
                    mm.then_inc(at_mm, 1)
                if live(w):
                    scores_n(w, 3)
                project_out(s, 1)
                if number(s) == STEPS + 5:
                    pe.wait_ge(exp_done, 5 * STEPS)
                    x2_transposed(0)
                if live(m):
                    scores_t(m, 3)
                if live(a):
                    attend(a, 0)
                if live(w):
                    scores_n(w, 4)
                if live(a):
                    attend(a, 1)
                project_out(s, 2)
                if live(m):
                    scores_t(m, 4)
                project_out(s, 3)

            pipeline(pe, step, prepare)

            def router(b):
                pe.wait_ge(x2l_done, b + 1)
                if b == B // 2:
                    pe.wait_ge(x1_done, B)
                for t in range(QT * b, QT * b + QT):
                    tok = slice(P * t, P * t + P)
                    a = E * (t % (TILES // 2))
                    three(bank[ROUT_BANK[b // 2]][:, a:a + E], xTh[:, tok], xTl[:, tok], routh, routl).then_inc(rout_mm, 1)

            last = (PAIRS - 1, STORE + B)
            x2_transposed(1)
            project_out(last, 0)
            pe.wait_ge(mrow_done, STEPS)
            router(0)
            project_out(last, 1)
            project_out(last, 2)
            x2_transposed(2)
            project_out(last, 3)
            router(1)

            def prepare2(c):
                if c == 0:
                    pe.wait_ge(x1_done, B - 1)
                if c == 2:
                    router(2)
                    x2_transposed(B - 1)
                if c == 3:
                    router(B - 1)

            def up(n):
                e, b = where(n)
                rows = slice(S * b, S * b + S)
                if isinstance(e, int) and e == 0:
                    pe.wait_ge(x2l_done, b + 1)
                wait(pe, h_done, count(n, 1, -1))
                for i in range(2):
                    cs = slice(P * i, P * i + P)
                    three(bank[2 * i + n[1] % 2][:, :], uph[:, e, cs], upl[:, e, cs],
                          xTh[:, rows], xTl[:, rows]).then_inc(up_mm, 1)

            def down(m):
                e, b = where(m)
                pe.wait_ge(hl_done, count(m, 1, 1))
                wait(pe, acc_done, count(m, 4, -4))
                for t in range(QT):
                    tok = slice(P * t, P * t + P)
                    mm = three(bank[6 + m[1] % 2][:, tok], hh[:, m[1] % 4, tok], hl[:, m[1] % 4, tok],
                               dnh[:, e, :], dnl[:, e, :])
                mm.then_inc(dn_mm, 1)

            def moe(n):
                if live(n):
                    up(n)
                m = minus(n, DOWN)
                if live(m):
                    down(m)

            pe.wait_ge(w2l_done, 4)
            pipeline_moe(pe, moe, DOWN, prepare2)


_INS = ['L0_attn_x', 'L0_attn_Q_w', 'L0_attn_Q_b', 'L0_attn_K_w', 'L0_attn_K_b', 'L0_attn_V_w', 'L0_attn_V_b',
        'L0_attn_O_w', 'L0_attn_O_b', 'L0_ffn_router_w', 'L0_ffn_up_proj', 'L0_ffn_down_proj']
_OUTS = [((4, 512, 128), 'float32')]


def kernel(**inputs):
    import numpy as _np
    import concourse.bacc as _bacc
    from concourse import mybir as _mybir
    from concourse.bass_utils import run_bass_kernel_spmd as _run

    nc = _bacc.Bacc("TRN2", target_bir_lowering=False, num_devices=1)
    arrays, args = {}, []
    for name in _INS:
        a = _np.ascontiguousarray(inputs[name])
        arrays[f"in_{name}_dram"] = a
        args.append(nc.dram_tensor(f"in_{name}_dram", a.shape, _mybir.dt.from_np(a.dtype), kind="ExternalInput").ap())
    for i, (shape, dtype) in enumerate(_OUTS):
        dt = _mybir.dt.from_np(_np.dtype(dtype))
        args.append(nc.dram_tensor(f"out_{i}_dram", shape, dt, kind="ExternalOutput").ap())
    build(nc, *args)
    r = _run(nc, [arrays], core_ids=[0])
    got = tuple(r.results[0][f"out_{i}_dram"] for i in range(len(_OUTS)))
    return got[0]
```
